# Optimizing a Trainium2 kernel written in Bass

```python
import numpy as np
import jax
import jax.numpy as jnp

def _softmax(x, axis=-1):
    return jax.nn.softmax(x, axis=axis)

def _gelu(x):
    return jax.nn.gelu(x, approximate=True)

def _silu(x):
    return jax.nn.silu(x)

def _sigmoid(x):
    return jax.nn.sigmoid(x)

def _layernorm(x, axis=-1, eps=1e-05):
    m = jnp.mean(x, axis=axis, keepdims=True)
    v = jnp.var(x, axis=axis, keepdims=True)
    return (x - m) / jnp.sqrt(v + eps)

def _scatter_add(tgt, idx, src, axis=0):
    return tgt.at[idx].add(src)

def _segment_sum(src, seg, n):
    return jax.ops.segment_sum(src, seg, n)
kernel_name = 'mk_gnn_ffn_d1_gnn_r8_dd4e93'

def setup_inputs(seed: int=0):
    np.random.seed(seed)
    _w = jnp.asarray

    def _rec_inputs():
        import jax
        import jax.numpy as jnp
        _gk = jax.random.key(seed)
        x = -0.0003713 + 1 * jax.random.normal(jax.random.fold_in(_gk, 1), (6250, 256), jnp.float32)
        src = jax.random.randint(jax.random.fold_in(_gk, 2), (100000,), 0, 6250, jnp.int32)
        dst = jax.random.randint(jax.random.fold_in(_gk, 3), (100000,), 0, 6250, jnp.int32)
        _o = jnp.argsort(dst, stable=True)
        src = src[_o]
        dst = dst[_o]
        edge_weight = jax.random.uniform(jax.random.fold_in(_gk, 12), (100000,), jnp.float32, 0.0, 0.999999)
        return (x, src, dst, edge_weight)
    x, src, dst, edge_weight = _rec_inputs()

    def _L0_gnn_setup():
        import jax, jax.numpy as jnp
        import numpy as np
        N = 6250
        D = 256
        E = 200000
        BN_EPS = 1e-05

        def gcn_conv(x, src, dst, w, W, b, n):
            xw = x @ W
            deg = jax.ops.segment_sum(w, dst, num_segments=n)
            dinv = jnp.where(deg > 0, jax.lax.rsqrt(deg), 0.0)
            norm = dinv[src] * w * dinv[dst]
            out = jax.ops.segment_sum(xw[src] * norm[:, None], dst, num_segments=n)
            return out + b
        key = jax.random.key(seed)
        ks = jax.random.split(key, 9)
        x = jax.random.normal(ks[0], (N, D), dtype=jnp.float32)
        edge_index = jax.random.randint(ks[1], (2, E), 0, N, dtype=jnp.int64)
        edge_weight = jax.random.uniform(ks[2], (E,), dtype=jnp.float32)
        s = 1.0 / np.sqrt(D)
        W1 = jax.random.uniform(ks[3], (D, D), minval=-s, maxval=s, dtype=jnp.float32)
        b1 = jnp.zeros((D,), dtype=jnp.float32)
        W2 = jax.random.uniform(ks[4], (D, D), minval=-s, maxval=s, dtype=jnp.float32)
        b2 = jnp.zeros((D,), dtype=jnp.float32)
        gamma = jnp.ones((D,), dtype=jnp.float32)
        beta = jnp.zeros((D,), dtype=jnp.float32)
        return {'x': x, 'edge_index': edge_index, 'edge_weight': edge_weight, 'W1': W1, 'b1': b1, 'W2': W2, 'b2': b2, 'gamma': gamma, 'beta': beta}
    _L0_gnn_all = _L0_gnn_setup()
    _L0_gnn_in = {k: v for k, v in _L0_gnn_all.items() if k in ('W1', 'b1', 'W2', 'b2', 'gamma', 'beta')}
    del _L0_gnn_all

    def _L0_ffn_setup():
        import jax, jax.numpy as jnp
        import numpy as np
        B, T, D, H, E = (16, 512, 256, 512, 8)
        key = jax.random.key(seed)
        ks = jax.random.split(key, 5)
        x = jax.random.normal(ks[0], (B, T, D), dtype=jnp.float32)
        gate_w = jax.random.normal(ks[1], (D, E), dtype=jnp.float32) * 0.02
        gate_b = jnp.zeros((E,), dtype=jnp.float32)
        W1 = jax.random.normal(ks[2], (E, D, H), dtype=jnp.float32) * 0.02
        b1 = jnp.zeros((E, H), dtype=jnp.float32)
        W2 = jax.random.normal(ks[3], (E, H, D), dtype=jnp.float32) * 0.02
        b2 = jnp.zeros((E, D), dtype=jnp.float32)
        return {'x': x, 'gate_w': gate_w, 'gate_b': gate_b, 'W1': W1, 'b1': b1, 'W2': W2, 'b2': b2}
    _L0_ffn_all = _L0_ffn_setup()
    _L0_ffn_in = {k: v for k, v in _L0_ffn_all.items() if k in ('gate_w', 'gate_b', 'W1', 'b1', 'W2', 'b2')}
    del _L0_ffn_all
    return {'x': x, 'src': src, 'dst': dst, 'edge_weight': edge_weight, 'L0_gnn_W1': _L0_gnn_in['W1'], 'L0_gnn_b1': _L0_gnn_in['b1'], 'L0_gnn_W2': _L0_gnn_in['W2'], 'L0_gnn_b2': _L0_gnn_in['b2'], 'L0_gnn_gamma': _L0_gnn_in['gamma'], 'L0_gnn_beta': _L0_gnn_in['beta'], 'L0_ffn_gate_w': _L0_ffn_in['gate_w'], 'L0_ffn_gate_b': _L0_ffn_in['gate_b'], 'L0_ffn_W1': _L0_ffn_in['W1'], 'L0_ffn_b1': _L0_ffn_in['b1'], 'L0_ffn_W2': _L0_ffn_in['W2'], 'L0_ffn_b2': _L0_ffn_in['b2']}

def reference(x, src, dst, edge_weight, L0_gnn_W1, L0_gnn_b1, L0_gnn_W2, L0_gnn_b2, L0_gnn_gamma, L0_gnn_beta, L0_ffn_gate_w, L0_ffn_gate_b, L0_ffn_W1, L0_ffn_b1, L0_ffn_W2, L0_ffn_b2):
    import jax
    import jax.numpy as jnp

    def _L0_gnn_ref(x, edge_index, edge_weight, W1, b1, W2, b2, gamma, beta):
        import jax, jax.numpy as jnp
        import numpy as np
        N = 6250
        D = 256
        E = 200000
        BN_EPS = 1e-05

        def gcn_conv(x, src, dst, w, W, b, n):
            xw = x @ W
            deg = jax.ops.segment_sum(w, dst, num_segments=n)
            dinv = jnp.where(deg > 0, jax.lax.rsqrt(deg), 0.0)
            norm = dinv[src] * w * dinv[dst]
            out = jax.ops.segment_sum(xw[src] * norm[:, None], dst, num_segments=n)
            return out + b
        n = x.shape[0]
        loop = jnp.arange(n, dtype=edge_index.dtype)
        src = jnp.concatenate([edge_index[0], loop])
        dst = jnp.concatenate([edge_index[1], loop])
        w = jnp.concatenate([edge_weight, jnp.ones((n,), dtype=edge_weight.dtype)])
        identity = x
        out = gcn_conv(x, src, dst, w, W1, b1, n)
        out = jax.nn.relu(out)
        out = gcn_conv(out, src, dst, w, W2, b2, n)
        mean = out.mean(axis=0)
        var = out.var(axis=0)
        out = (out - mean) * jax.lax.rsqrt(var + BN_EPS) * gamma + beta
        out = out + identity
        return jax.nn.relu(out)

    def _L0_ffn_ref(x, gate_w, gate_b, W1, b1, W2, b2):
        import jax, jax.numpy as jnp
        import numpy as np
        B, T, D, H, E = (16, 512, 256, 512, 8)
        Bb, Tt, Dd = x.shape
        Ee = gate_w.shape[1]
        xf = x.reshape(-1, Dd)
        N = xf.shape[0]
        logits = xf @ gate_w + gate_b
        probs = jax.nn.softmax(logits, axis=-1)
        top2_vals, top2_idx = jax.lax.top_k(probs, 2)
        cw = jnp.zeros((N, Ee), dtype=xf.dtype).at[jnp.arange(N)[:, None], top2_idx].add(top2_vals)

        def step(acc, params):
            w1, bb1, w2, bb2, we = params
            h = jax.nn.gelu(xf @ w1 + bb1, approximate=False)
            y = h @ w2 + bb2
            return (acc + we[:, None] * y, None)
        out, _ = jax.lax.scan(step, jnp.zeros_like(xf), (W1, b1, W2, b2, cw.T))
        return out.reshape(Bb, Tt, Dd)
    edge_index = jnp.stack([src, dst])
    x = x + _L0_gnn_ref(_layernorm(x, axis=-1), edge_index, edge_weight, L0_gnn_W1, L0_gnn_b1, L0_gnn_W2, L0_gnn_b2, L0_gnn_gamma, L0_gnn_beta)
    x = x + _L0_ffn_ref(_layernorm(x, axis=-1)[None], L0_ffn_gate_w, L0_ffn_gate_b, L0_ffn_W1, L0_ffn_b1, L0_ffn_W2, L0_ffn_b2)[0]
    return x

_drawn_inputs = setup_inputs


def setup_inputs(seed=0):
    import zlib

    import numpy as np

    out = dict(_drawn_inputs(seed))
    spreads = {'L0_gnn_b1': (0.0, 0.1),
     'L0_gnn_b2': (0.0, 0.8),
     'L0_gnn_gamma': (1.0, 0.2),
     'L0_gnn_beta': (0.0, 0.1),
     'L0_ffn_gate_b': (0.0, 0.739),
     'L0_ffn_b1': (0.0, 0.8),
     'L0_ffn_b2': (0.0, 0.538)}
    factors = {'L0_ffn_gate_w': 3.429, 'L0_ffn_W1': 4.916, 'L0_ffn_W2': 4.621}
    for name, (base, spread) in spreads.items():
        noise = np.random.default_rng([zlib.crc32(name.encode()), seed]).standard_normal(out[name].shape)
        drawn = base * np.exp(spread * noise) if base else spread * noise
        out[name] = jnp.asarray(drawn.astype(out[name].dtype))
    for name, factor in factors.items():
        out[name] = (out[name] * factor).astype(out[name].dtype)
    return out
```

```python
from contextlib import ExitStack, contextmanager

import concourse.bass as bass
from concourse import mybir

F32 = mybir.dt.float32
I32 = mybir.dt.int32
ALU = mybir.AluOpType
ACT = mybir.ActivationFunctionType
AX_X = mybir.AxisListType.X

P = 128
CH = 7
GT = 14
OH = 8
WIN = 448
LN_EPS = 1e-05
BN_EPS = 1e-05


class Chain:

    def __init__(self, eng, sem):
        self.eng, self.sem, self.n, self.steps = eng, sem, 0, 0

    def __call__(self, ins):
        ins.then_inc(self.sem, 1)
        self.n, self.steps = self.n + 1, self.steps + 1
        self.eng.wait_ge(self.sem, self.n)

    @contextmanager
    def loop(self, count, steps):
        base, before = self.n, self.steps
        with self.eng.Fori(0, count) as i:
            self.n = i * steps + base
            yield i
            assert self.steps - before == steps, (self.steps - before, steps)
        self.n = base + steps * count


def gnn_ffn(nc, x, src, dst, edge_weight, g_W1, g_b1, g_W2, g_b2, g_gamma, g_beta,
            gate_w, gate_b, e_W1, e_b1, e_W2, e_b2, out):
    N, D = x.shape
    E = src.shape[0]
    NX, _, H = e_W1.shape
    KC = D // P
    HC = H // P
    NT = -(-N // P)
    TAIL = N - (NT - 1) * P
    NP = NT * P
    NCH = NT // CH
    ET = -(-E // (P * 2 * GT)) * 2 * GT
    NG = ET // GT
    RB = -(-(ET + 2 * GT) // P)
    EC = RB * P
    EFULL = E // P // P
    EROWS = E // P - EFULL * P
    EREST = E - (EFULL * P + EROWS) * P
    NW = NP // WIN
    FT = (2 * N + NX * (P - 1)) // P
    assert NT == NCH * CH and NP == NW * WIN and EFULL == RB - 1 and ET % (2 * OH) == 0 and KC == 2

    y_tab = [nc.dram_tensor(f"conv{n}_rows", (NP, D), F32, kind="Internal").ap() for n in range(2)]
    routed = nc.dram_tensor("routed_rows", ((FT + 2) * P, D), F32, kind="Internal").ap()
    expert_out = nc.dram_tensor("expert_rows", (FT * P, D), F32, kind="Internal").ap()

    with ExitStack() as ctx:
        def sb(name, cols, dt=F32):
            return ctx.enter_context(nc.sbuf_tensor(name, [P, cols], dt))

        def sem(name):
            return ctx.enter_context(nc.semaphore(name))

        X = sb("X", NT * D)
        ACC = sb("ACC", KC * NP)
        arena = sb("arena", NX * (KC * H + HC * D))
        acc = ACC[:, :].rearrange("p (c n) -> p c n", c=KC)

        edge_row = [arena[:, n * EC:(n + 1) * EC] for n in range(8)]
        src_row, dst_row, w_row = edge_row[0].bitcast(I32), edge_row[1].bitcast(I32), edge_row[2]
        src_rowf, dst_rowf = edge_row[3], edge_row[4]
        dst_lo, dst_hi, dint = edge_row[5], edge_row[6], edge_row[7].bitcast(I32)
        at = 2 * GT * D
        G = arena[:, 0:at]
        S = arena[:, at:at + 2 * GT * P]
        YR = arena[:, at:at + 2 * CH * D]
        at += 2 * GT * P
        LO = arena[:, at:at + 2 * OH * P]
        at += 2 * OH * P
        HI = arena[:, at:at + 2 * OH * NT]
        w1e = arena[:, 0:NX * KC * H]
        w2e = arena[:, NX * KC * H:NX * (KC * H + HC * D)]
        Y12 = arena[:, 0:2 * 2 * CH * D]
        OR = arena[:, 4 * CH * D:6 * CH * D]
        XN = ACC[:, 0:2 * CH * D]
        at = 2 * CH * D
        xs = ACC[:, at:at + 4 * D]
        at += 4 * D
        xsT = ACC[:, at:at + 2 * D]
        at += 2 * D
        hT = ACC[:, at:at + 2 * H]
        at += 2 * H
        ys = ACC[:, at:at + 2 * D]
        at += 2 * D
        T8 = NT * NX
        prob, sel1, sel2, sA, sB = [ACC[:, at + n * T8:at + (n + 1) * T8] for n in range(5)]
        at += 5 * T8
        pos, texp_f = ACC[:, at:at + 2 * NT], ACC[:, at + 2 * NT:at + 2 * NT + FT]
        at += 2 * NT + FT
        pos_s, pos_g, texp_i = [ACC[:, at + n * P:at + n * P + w].bitcast(I32)
                                for n, w in enumerate((2 * NT, 2 * NT, FT))]
        at += 3 * P
        w1s = ACC[:, at:at + 2 * KC * H]
        assert at + 2 * KC * H <= KC * NP

        srcT = sb("srcT", EC, I32)
        dstT, wT, dst_rel = [sb(n, EC) for n in ("dstT", "wT", "dst_rel")]
        base_f, base_i = sb("base_f", NG), sb("base_i", NG, I32)
        bad, flag_i = sb("bad", 4), sb("flag_i", 4, I32)
        stg = sb("stg", 2 * GT, I32)
        gstg = sb("gstg", 2, I32)
        iota = sb("iota", WIN)
        offs = sb("offs", NW)
        dcol = sb("dcol", NW)
        ident, before, ones, not_pad = [sb(n, P) for n in ("ident", "before", "ones", "not_pad")]
        zeros = sb("zeros", D)
        turns = sb("turns", 2)
        rank8, trash = sb("rank8", NX), sb("trash", 1)
        tile_at = sb("tile_at", FT)
        W1g, W2g = sb("W1g", KC * D), sb("W2g", KC * D)
        gw = sb("gw", KC * NX)
        b1g, b2g, gam, bet = [sb(n, D) for n in ("b1g", "b2g", "gam", "bet")]
        gb = sb("gb", NX)
        b2e = sb("b2e", NX * D)
        b1e = sb("b1e", NX * HC)
        deg, dinv, mask, rstd, nmr, sc, nb = [sb(n, NT) for n in ("deg", "dinv", "mask", "rstd", "nmr", "sc", "nb")]
        stats, mv7, mv = sb("stats", CH * 6), sb("mv7", CH * 2), sb("mv", NT * 2)
        tmp = sb("tmp", 2 * D)
        ln = sb("ln", 2 * D)
        mean_b, scale_b = sb("mean_b", D), sb("scale_b", D)
        b1rows, sd_b = tmp, mean_b
        red, cw1, cw2 = sb("red", NT), sb("cw1", NT), sb("cw2", NT)
        valid = sb("valid", NT)
        cap, capx, endx = sb("cap", NX), sb("capx", NX), sb("endx", NX)
        cap_i = sb("cap_i", NX, I32)
        pstg = sb("pstg", 4 * CH, I32)
        dscr = sb("dscr", 1)

        psum = ctx.enter_context(nc.psum_tensor("psum", [P, 8, 512], F32))

        def bank(b, cols, n=1):
            return psum[:, b:b + n, :].rearrange("p b f -> p (b f)")[:, 0:cols]

        ld_edges, ld_const, ld_exp = sem("ld_edges"), sem("ld_const"), sem("ld_exp")
        ld_x = [sem(f"ld_x{n}") for n in range(NCH)]
        r_pad, x_pad, zeros_set = sem("r_pad"), sem("x_pad"), sem("zeros_set")
        routed_zeroed = sem("routed_zeroed")
        consts_set, pool_chain = sem("consts_set"), sem("pool_chain")
        dve_chain, act_chain = sem("dve_chain"), sem("act_chain")
        edge_f, edges_turned = sem("edge_f"), sem("edges_turned")
        dstT_set, base_bc, bad_set, bad_sum, flag_set = [sem(n) for n in ("dstT_set", "base_bc", "bad_set", "bad_sum", "flag_set")]
        b1_turned = sem("b1_turned")
        oh_free, hi_ready, deg_done = sem("oh_free"), sem("hi_ready"), sem("deg_done")
        deg_var, deg_sd, sc_set = sem("deg_var"), sem("deg_sd"), sem("sc_set")
        y_ready, y_turned, y_copied = sem("y_ready"), sem("y_turned"), sem("y_copied")
        y_stored = [sem(f"y_stored{n}") for n in range(2)]
        staged, turn = sem("staged"), sem("turn")
        gathered = [sem(f"gathered{n}") for n in range(2 * GT)]
        s_ready, summed, added, agg_done = sem("s_ready"), sem("summed"), sem("added"), sem("agg_done")
        gen_staged, gen_turn, gen_gathered = sem("gen_staged"), sem("gen_turn"), sem("gen_gathered")
        sem_gen_chain = sem("gen_chain")
        gen_s, gen_summed, gen_added = sem("gen_s"), sem("gen_summed"), sem("gen_added")
        lin_done, lin_used = sem("lin_done"), sem("lin_used")
        sum_done, centred, sq_ready, sq_used = sem("sum_done"), sem("centred"), sem("sq_ready"), sem("sq_used")
        bn_var, bn_sd, ln_ready, lb_ready, lb_used = [sem(n) for n in ("bn_var", "bn_sd", "ln_ready", "lb_ready", "lb_used")]
        ln2_var, ln2_sd, ln2_set = sem("ln2_var"), sem("ln2_sd"), sem("ln2_set")
        n_ready, n_turned, n_copied, logit_done = [sem(n) for n in ("n_ready", "n_turned", "n_copied", "logit_done")]
        lmax_set, exp_done = sem("lmax_set"), sem("exp_done")
        member_set, rank_done, pos_set = sem("member_set"), sem("rank_done"), sem("pos_set")
        xn_ready, pos_staged = sem("xn_ready"), sem("pos_staged")
        scattered = [sem(f"scattered{n}") for n in range(2)]
        xs_in = [sem(f"xs_in{n}") for n in range(4)]
        f_turned, f_copied, h_done, h_act, o_done, ys_ready = [sem(n) for n in ("f_turned", "f_copied", "h_done", "h_act", "o_done", "ys_ready")]
        w1_staged = sem("w1_staged")
        ys_out = [sem(f"ys_out{n}") for n in range(2)]
        back = [sem(f"back{n}") for n in range(2)]
        o_ready = sem("o_ready")
        o_out = [sem(f"o_out{n}") for n in range(2)]

        LOADS = 9
        HALVES = ET // OH
        STAGED = NG + 2
        Q = NT
        SLOT_CH = [(NCH + 1) // 2, NCH // 2]
        FFN_LOOP = (FT - 2) // 2

        def prior(q, j):
            return q + 1 if j == 0 else q

        def rows_of(table, c, tiles=CH):
            return table[bass.ds(c * (CH * P), tiles * P), :].rearrange("(t p) d -> p t d", p=P)

        def tile3(ap, n=CH):
            return ap.rearrange("p (t d) -> p t d", t=n)

        with nc.Block() as block:

            @block.sync
            def _(sp):
                for a, r in ((src, src_row), (dst, dst_row), (edge_weight, w_row)):
                    sp.dma_start(r[:, 0:EFULL * P].rearrange("p (b e) -> p b e", b=EFULL),
                                 a[0:EFULL * P * P].rearrange("(b p e) -> p b e", p=P, e=P)).then_inc(ld_edges, 16)
                sp.wait_ge(r_pad, 3)
                for a, r in ((src, src_row), (dst, dst_row), (edge_weight, w_row)):
                    e0 = EFULL * P * P
                    sp.dma_start(r[0:EROWS, EFULL * P:EC],
                                 a[e0:e0 + EROWS * P].rearrange("(p e) -> p e", e=P)).then_inc(ld_edges, 16)
                    sp.dma_start(r[EROWS:EROWS + 1, EFULL * P:EFULL * P + EREST],
                                 a[e0 + EROWS * P:E].rearrange("(p e) -> p e", p=1)).then_inc(ld_edges, 16)
                for c in range(NCH):
                    if c < NCH - 1:
                        sp.dma_start(tile3(X[:, c * CH * D:(c + 1) * CH * D]), rows_of(x, c)).then_inc(ld_x[c], 16)
                    else:
                        sp.wait_ge(x_pad, 1)
                        t0 = (NT - 1) * D
                        sp.dma_start(tile3(X[:, c * CH * D:t0], CH - 1), rows_of(x, c, CH - 1)).then_inc(ld_x[c], 16)
                        sp.dma_start(X[0:TAIL, t0:t0 + D], x[(NT - 1) * P:N, :]).then_inc(ld_x[c], 16)
                sp.wait_ge(zeros_set, 1)
                sp.dma_start(routed.rearrange("(t p) d -> p t d", p=P),
                             zeros[:, :].unsqueeze(1).broadcast_to([P, FT + 2, D])).then_inc(routed_zeroed, 16)

                for layer in range(2):
                    for c in range(NCH):
                        sp.wait_ge(y_ready, Q * layer + CH * (c + 1))
                        r0 = (c % 2) * CH * D
                        sp.dma_start(rows_of(y_tab[layer], c), tile3(YR[:, r0:r0 + CH * D])).then_inc(y_stored[c % 2], 16)

                sp.wait_ge(agg_done, 2)
                for e in range(NX):
                    sp.dma_start(w1e[:, e * KC * H:(e + 1) * KC * H].rearrange("p (c h) -> p c h", c=KC),
                                 e_W1[e].rearrange("(c p) h -> p c h", p=P)).then_inc(ld_exp, 16)
                    sp.dma_start(w2e[:, e * HC * D:(e + 1) * HC * D].rearrange("p (c d) -> p c d", c=HC),
                                 e_W2[e].rearrange("(c p) d -> p c d", p=P)).then_inc(ld_exp, 16)

                for n in range(2):
                    sp.wait_ge(scattered[n], 16 * 2 * CH * SLOT_CH[n])

                def load_xs(j, slot):
                    sp.dma_start(xs[:, slot * D:(slot + 1) * D],
                                 routed[bass.ds(j * P, P), :]).then_inc(xs_in[slot], 16)

                def store_ys(j, slot):
                    sp.wait_ge(ys_ready, j + 1)
                    sp.dma_start(expert_out[bass.ds(j * P, P), :],
                                 ys[:, slot * D:(slot + 1) * D]).then_inc(ys_out[slot], 16)

                for j in range(4):
                    load_xs(j, j)
                whole = (FT - 4) // 4
                with sp.Fori(0, whole) as i:
                    for u in range(4):
                        sp.wait_ge(f_turned, i * 4 + (u + 1))
                        load_xs(i * 4 + (u + 4), u)
                        store_ys(i * 4 + u, u % 2)
                for j in range(4 * whole, FT):
                    if j + 4 < FT:
                        sp.wait_ge(f_turned, j + 1)
                        load_xs(j + 4, j % 4)
                    store_ys(j, j % 2)

                for c in range(NCH):
                    sp.wait_ge(o_ready, CH * (c + 1))
                    r0 = (c % 2) * CH * D
                    if c < NCH - 1:
                        sp.dma_start(rows_of(out, c), tile3(OR[:, r0:r0 + CH * D])).then_inc(o_out[c % 2], 16)
                    else:
                        t0 = r0 + (CH - 1) * D
                        sp.dma_start(rows_of(out, c, CH - 1), tile3(OR[:, r0:t0], CH - 1)).then_inc(o_out[c % 2], 16)
                        sp.dma_start(out[(NT - 1) * P:N, :], OR[0:TAIL, t0:t0 + D]).then_inc(o_out[c % 2], 16)
                for n in range(2):
                    sp.wait_ge(o_out[n], 16 * (SLOT_CH[n] + ((NCH - 1) % 2 == n)))

            @block.gpsimd
            def _(pool):
                chain = Chain(pool, pool_chain)
                g = nc.gpsimd
                g.iota(iota[:, :], [[1, WIN]], base=0, channel_multiplier=0, allow_small_or_imprecise_dtypes=True)
                g.iota(offs[:, :], [[-WIN, NW]], base=0, channel_multiplier=0, allow_small_or_imprecise_dtypes=True)
                g.iota(rank8[:, :], [[-1, NX]], base=NX, channel_multiplier=0, allow_small_or_imprecise_dtypes=True)
                g.iota(trash[:, :], [[0, 1]], base=FT * P, channel_multiplier=1, allow_small_or_imprecise_dtypes=True)
                g.iota(tile_at[:, :], [[P, FT]], base=0, channel_multiplier=0, allow_small_or_imprecise_dtypes=True)
                g.memset(ident[:, :], 0.0)
                g.memset(before[:, :], 0.0)
                g.memset(ones[:, :], 1.0)
                chain(g.memset(not_pad[:, :], 0.0))
                g.affine_select(out=ident[:, :], in_=ident[:, :], compare_op=ALU.not_equal, fill=1.0, base=0,
                                pattern=[[-1, P]], channel_multiplier=1)
                g.affine_select(out=before[:, :], in_=before[:, :], compare_op=ALU.is_ge, fill=1.0, base=0,
                                pattern=[[-1, P]], channel_multiplier=1)
                g.affine_select(out=not_pad[:, :], in_=not_pad[:, :], compare_op=ALU.is_gt, fill=-1.0, base=TAIL,
                                pattern=[[0, P]], channel_multiplier=-1).then_inc(consts_set, 1)

                def take_turn(sem_turn, n):
                    pool.wait_ge(sem_turn, n)
                    g.tensor_tensor(turns[:, 0:1], zeros[:, 0:1], zeros[:, 1:2], ALU.add).then_inc(sem_turn, 1)

                pool.sem_inc(turn, 1)
                pool.sem_inc(gen_turn, 1)
                pool.wait_ge(zeros_set, 1)
                pool.wait_ge(flag_set, 1)
                general = pool.value_load(flag_i[0:1, 0:1], min_val=0, max_val=1)
                for layer in range(2):
                    for n in range(2):
                        pool.wait_ge(y_stored[n], 16 * SLOT_CH[n] * (layer + 1))
                    with pool.If(general == 0):
                        with pool.Fori(0, NG // 2) as i:
                            for h in range(2):
                                pool.wait_ge(staged, i * 2 + (STAGED * layer + h + 1))
                                take_turn(turn, i * 2 + (NG * layer + h + 1))
                                for j in range(GT):
                                    n = h * GT + j
                                    pool.indirect_dma_start(
                                        G[:, n * D:(n + 1) * D], None, y_tab[layer],
                                        bass.IndirectOffsetOnAxis(stg[:, n:n + 1], 0)).then_inc(gathered[n], 16)
                    with pool.Else():
                        with pool.Fori(0, ET) as i:
                            pool.wait_ge(gen_staged, i + (ET * layer + 1))
                            take_turn(gen_turn, i + (ET * layer + 1))
                            pool.indirect_dma_start(
                                G[:, 0:D], None, y_tab[layer],
                                bass.IndirectOffsetOnAxis(gstg[:, 0:1], 0)).then_inc(gen_gathered, 16)

                with pool.Fori(0, NCH) as c:
                    for j in range(CH):
                        q = c * CH + j
                        pool.wait_ge(ln_ready, q + 1)
                        a = ln[:, (j % 2) * D:(j % 2 + 1) * D]
                        g.tensor_tensor(a, a, bet[:, :], ALU.add).then_inc(lb_ready, 1)

                pool.wait_ge(routed_zeroed, 16)
                for c in range(NCH):
                    pool.wait_ge(pos_staged, 2 if c == 0 else c + 1)
                    for j in range(CH):
                        n = (c % 2) * CH + j
                        pool.wait_ge(xn_ready, CH * c + j + 1)
                        for k in range(2):
                            pool.indirect_dma_start(
                                routed, bass.IndirectOffsetOnAxis(pstg[:, 2 * n + k:2 * n + k + 1], 0),
                                XN[:, n * D:(n + 1) * D], None).then_inc(scattered[c % 2], 16)

                for n in range(2):
                    pool.wait_ge(ys_out[n], 16 * ((FT + 1 - n) // 2))
                for c in range(NCH):
                    pool.wait_ge(pos_staged, NCH + c + 1)
                    if c >= 2:
                        pool.wait_ge(o_ready, CH * (c - 1))
                    for j in range(CH):
                        n = (c % 2) * CH + j
                        for k in range(2):
                            m = 2 * n + k
                            pool.indirect_dma_start(
                                Y12[:, m * D:(m + 1) * D], None, expert_out,
                                bass.IndirectOffsetOnAxis(pstg[:, m:m + 1], 0)).then_inc(back[c % 2], 16)

            @block.scalar
            def _(act):
                chain = Chain(act, act_chain)
                a = nc.scalar
                act.dma_start(W1g[:, :].rearrange("p (c d) -> p c d", c=KC),
                              g_W1.rearrange("(c p) d -> p c d", p=P)).then_inc(ld_const, 16)
                act.dma_start(W2g[:, :].rearrange("p (c d) -> p c d", c=KC),
                              g_W2.rearrange("(c p) d -> p c d", p=P)).then_inc(ld_const, 16)
                act.dma_start(gw[:, :].rearrange("p (c e) -> p c e", c=KC),
                              gate_w.rearrange("(c p) e -> p c e", p=P)).then_inc(ld_const, 16)
                for to, row in ((b1g, g_b1), (b2g, g_b2), (gam, g_gamma), (bet, g_beta), (gb, gate_b)):
                    act.dma_start(to[:, :], row.partition_broadcast(P)).then_inc(ld_const, 16)
                act.dma_start(b2e[:, :], e_b2.rearrange("e d -> (e d)").partition_broadcast(P)).then_inc(ld_const, 16)
                act.dma_start(b1rows[0:NX * HC, 0:P],
                              e_b1.rearrange("e (c p) -> (e c) p", p=P)).then_inc(ld_const, 16)

                act.wait_ge(deg_var, 2)
                a.activation(deg[:, :], deg[:, :], ACT.Sqrt).then_inc(deg_sd, 1)
                a.activation(rstd[:, :], rstd[:, :], ACT.Sqrt).then_inc(deg_sd, 1)

                act.wait_ge(sc_set, 1)
                for c in range(NCH):
                    for j in range(CH):
                        n, t = (c % 2) * CH + j, CH * c + j
                        if c >= 2 and j == 0:
                            act.wait_ge(y_stored[c % 2], 16 * (c // 2))
                            act.wait_ge(y_turned, 1 + CH * (c - 1))
                        a.activation(YR[:, n * D:(n + 1) * D], X[:, t * D:(t + 1) * D], ACT.Identity,
                                     bias=nb[:, t:t + 1], scale=sc[:, t:t + 1]).then_inc(y_ready, 1)

                for n in range(2):
                    act.wait_ge(y_stored[n], 16 * SLOT_CH[n])
                for c in range(NCH):
                    for j in range(CH):
                        n, t = (c % 2) * CH + j, CH * c + j
                        if c >= 2 and j == 0:
                            act.wait_ge(y_stored[c % 2], 16 * (SLOT_CH[c % 2] + c // 2))
                            act.wait_ge(y_turned, 1 + Q + CH * (c - 1))
                        act.wait_ge(lin_used, 1 + t + 1)
                        a.activation(YR[:, n * D:(n + 1) * D], tmp[:, (j % 2) * D:(j % 2 + 1) * D], ACT.Relu,
                                     scale=dinv[:, t:t + 1]).then_inc(y_ready, 1)

                with act.Fori(0, NCH) as c:
                    act.wait_ge(centred, c * 2 + 2)
                    for j in range(CH):
                        q = c * CH + j
                        act.wait_ge(sq_used, prior(q, j))
                        a.activation(tmp[:, (j % 2) * D:(j % 2 + 1) * D].rearrange("p (c n) -> p c n", c=KC),
                                     acc[:, :, bass.ds(q * P, P)], ACT.Square).then_inc(sq_ready, 1)
                act.wait_ge(bn_var, 1)
                a.activation(sd_b[:, :], sd_b[:, :], ACT.Sqrt).then_inc(bn_sd, 1)

                with act.Fori(0, NCH) as c:
                    for j in range(CH):
                        q = c * CH + j
                        act.wait_ge(lb_used, prior(q, j))
                        a.activation(ln[:, (j % 2) * D:(j % 2 + 1) * D], X[:, bass.ds(q * D, D)], ACT.Identity,
                                     bias=nmr[:, bass.ds(q, 1)], scale=rstd[:, bass.ds(q, 1)]).then_inc(ln_ready, 1)
                act.wait_ge(ln2_var, 1)
                a.activation(rstd[:, :], rstd[:, :], ACT.Sqrt).then_inc(ln2_sd, 1)

                act.wait_ge(ln2_set, 1)
                with act.Fori(0, NCH) as c:
                    for j in range(CH):
                        q = c * CH + j
                        act.wait_ge(n_turned, prior(q, j))
                        a.activation(tmp[:, (j % 2) * D:(j % 2 + 1) * D], X[:, bass.ds(q * D, D)], ACT.Identity,
                                     bias=nmr[:, bass.ds(q, 1)], scale=rstd[:, bass.ds(q, 1)]).then_inc(n_ready, 1)
                act.wait_ge(lmax_set, 1)
                a.activation(prob[:, :], prob[:, :], ACT.Exp).then_inc(exp_done, 1)

                for c in range(NCH):
                    if c >= 2:
                        act.wait_ge(scattered[c % 2], 16 * 2 * CH * (c // 2))
                    for j in range(CH):
                        n, t = (c % 2) * CH + j, CH * c + j
                        a.activation(XN[:, n * D:(n + 1) * D], X[:, t * D:(t + 1) * D], ACT.Identity,
                                     bias=nmr[:, t:t + 1], scale=rstd[:, t:t + 1]).then_inc(xn_ready, 1)

                def gelu(j, slot):
                    e = act.value_load(texp_i[0:1, bass.ds(j, 1)], min_val=0, max_val=NX - 1)
                    act.wait_ge(h_done, j + 1)
                    act.wait_ge(o_done, j)
                    for c in range(HC):
                        ins = a.activation(hT[:, slot * H + c * P:slot * H + (c + 1) * P],
                                           psum[:, 2 + slot, c * P:(c + 1) * P], ACT.Gelu,
                                           bias=b1e[:, bass.ds(e * HC + c, 1)])
                    ins.then_inc(h_act, 1)

                act.wait_ge(b1_turned, 2)
                gelu(0, 0)
                with act.Fori(0, (FT - 1) // 2) as i:
                    for u in range(2):
                        gelu(i * 2 + (u + 1), (u + 1) % 2)
                for j in range(1 + (FT - 1) // 2 * 2, FT):
                    gelu(j, j % 2)

            @block.vector
            def _(dve):
                chain, gen_chain = Chain(dve, dve_chain), Chain(dve, sem_gen_chain)
                v = nc.vector
                last0 = EFULL * P
                v.memset(src_row[:, last0:EC], 0).then_inc(r_pad, 1)
                v.memset(dst_row[:, last0:EC], N - 1).then_inc(r_pad, 1)
                v.memset(w_row[:, last0:EC], 0.0).then_inc(r_pad, 1)
                v.memset(X[:, (NT - 1) * D:NT * D], 0.0).then_inc(x_pad, 1)
                v.memset(zeros[:, :], 0.0).then_inc(zeros_set, 1)
                v.memset(valid[:, :], 1.0)
                dve.sem_inc(oh_free, 2)
                dve.sem_inc(y_copied, 1)
                dve.sem_inc(added, 2)
                dve.sem_inc(gen_added, 1)
                dve.sem_inc(lin_used, 1)
                dve.sem_inc(lb_used, 1)
                dve.sem_inc(n_copied, 1)

                dve.wait_ge(ld_edges, 16 * LOADS)
                v.tensor_copy(src_rowf, src_row).then_inc(edge_f, 1)
                v.tensor_copy(dst_rowf, dst_row).then_inc(edge_f, 1)
                dve.wait_ge(edges_turned, 1)
                v.tensor_copy(dstT[:, :], bank(0, EC, 2)).then_inc(dstT_set, 1)
                v.tensor_copy(dint[:, :], bank(0, EC, 2))
                dve.wait_ge(edges_turned, 2)
                chain(v.tensor_copy(wT[:, :], bank(2, EC, 2)))
                chain(v.tensor_scalar(dst_lo[:, :].bitcast(I32), dint[:, :], P - 1, None, ALU.bitwise_and))
                chain(v.tensor_scalar(dst_hi[:, :].bitcast(I32), dint[:, :], P.bit_length() - 1, None,
                                      ALU.logical_shift_right))
                v.tensor_copy(dst_rel[:, :], dst_lo[:, :].bitcast(I32))
                chain(v.tensor_copy(dint[:, :].bitcast(F32), dst_hi[:, :].bitcast(I32)))
                v.tensor_copy(dst_lo[:, :], dst_rel[:, :])
                chain(v.tensor_copy(dst_hi[:, :], dint[:, :].bitcast(F32)))
                dve.wait_ge(edges_turned, 3)
                v.tensor_copy(srcT[:, :], bank(4, EC, 2))

                dve.wait_ge(consts_set, 1)
                with dve.Fori(0, ET // (2 * OH)) as i:
                    for h in range(2):
                        dve.wait_ge(oh_free, i * 2 + (h + 1))
                        for j in range(OH):
                            n = h * OH + j
                            t = i * (2 * OH) + n
                            v.tensor_scalar(LO[:, n * P:(n + 1) * P], iota[:, 0:P], dst_lo[:, bass.ds(t, 1)], None,
                                            ALU.is_equal)
                            v.tensor_scalar(HI[:, n * NT:(n + 1) * NT], iota[:, 0:NT], dst_hi[:, bass.ds(t, 1)],
                                            wT[:, bass.ds(t, 1)], ALU.is_equal, ALU.mult).then_inc(hi_ready, 1)

                dve.wait_ge(base_bc, 1)
                chain(v.tensor_scalar(base_f[:, :], bank(6, NG), float(NP - P), None, ALU.min))
                v.tensor_copy(base_i[:, :], base_f[:, :])
                chain(v.tensor_tensor(dst_rel[:, 0:ET].rearrange("p (g t) -> p g t", t=GT),
                                      dstT[:, 0:ET].rearrange("p (g t) -> p g t", t=GT),
                                      base_f[:, :].unsqueeze(2).broadcast_to([P, NG, GT]), ALU.subtract))
                chain(v.tensor_reduce(bad[:, 0:1], dst_rel[:, 0:ET], AX_X, ALU.max))
                chain(v.tensor_reduce(bad[:, 1:2], dst_rel[:, 0:ET], AX_X, ALU.min))
                chain(v.tensor_scalar(bad[:, 2:3], bad[:, 0:1], float(P - 1), None, ALU.is_gt))
                chain(v.tensor_scalar(bad[:, 3:4], bad[:, 1:2], 0.0, bad[:, 2:3], ALU.is_lt, ALU.add))
                v.tensor_copy(dscr[:, :], bad[:, 3:4]).then_inc(bad_set, 1)
                dve.wait_ge(bad_sum, 1)
                chain(v.tensor_scalar(bad[:, 0:1], bank(6, 1), 0.5, None, ALU.is_gt))
                v.tensor_copy(flag_i[:, 0:1], bad[:, 0:1]).then_inc(flag_set, 1)
                dve.wait_ge(b1_turned, 1)
                chain(v.tensor_copy(b1e[:, :], bank(5, NX * HC)))

                def moments(c):
                    for j in range(CH):
                        v.bn_stats(stats[:, 6 * j:6 * j + 6], X[:, bass.ds((c * CH + j) * D, D)])
                    chain(v.tensor_copy(dscr[:, :], zeros[:, 0:1]))
                    for j in range(CH):
                        v.bn_aggr(mv7[:, 2 * j:2 * j + 2], stats[:, 6 * j:6 * j + 6])
                    chain(v.tensor_copy(dscr[:, :], zeros[:, 0:1]))
                    chain(v.tensor_copy(mv[:, bass.ds(c * 2 * CH, 2 * CH)], mv7[:, :]))

                def mean_var():
                    m = mv[:, :].rearrange("p (t k) -> p t k", k=2)
                    return m[:, :, 0], m[:, :, 1]

                for c in range(NCH):
                    dve.wait_ge(ld_x[c], 32 if c == NCH - 1 else 16)
                for c in range(NCH):
                    moments(c)
                mean, var = mean_var()
                chain(v.tensor_scalar(rstd[:, :], var, LN_EPS, None, ALU.add))
                dve.wait_ge(deg_done, 1)
                chain(v.tensor_scalar(mask[:, :], bank(7, NT), 0.0, None, ALU.is_gt))
                v.tensor_scalar(deg[:, :], bank(7, NT), 1e-30, None, ALU.max).then_inc(deg_var, 1)
                v.tensor_copy(dscr[:, :], zeros[:, 0:1]).then_inc(deg_var, 1)
                dve.wait_ge(deg_sd, 2)
                chain(v.reciprocal(dinv[:, :], deg[:, :]))
                chain(v.tensor_tensor(dinv[:, :], dinv[:, :], mask[:, :], ALU.mult))
                chain(v.reciprocal(mask[:, :], rstd[:, :]))
                chain(v.tensor_copy(rstd[:, :], mask[:, :]))
                chain(v.scalar_tensor_tensor(out=nmr[:, :], in0=mean, scalar=-1.0, in1=rstd[:, :], op0=ALU.mult, op1=ALU.mult))
                chain(v.tensor_tensor(sc[:, :], rstd[:, :], dinv[:, :], ALU.mult))
                v.tensor_tensor(nb[:, :], nmr[:, :], dinv[:, :], ALU.mult).then_inc(sc_set, 1)

                def copy_turned(layer, q, j):
                    dve.wait_ge(y_turned, q + (1 + Q * layer + 1))
                    v.tensor_copy(acc[:, :, bass.ds(q * P, P)],
                                  bank(j % 2, D).rearrange("p (c n) -> p c n", c=KC)).then_inc(y_copied, 1)

                with dve.Fori(0, NCH) as c:
                    for j in range(CH):
                        copy_turned(0, c * CH + j, j)

                general = dve.value_load(flag_i[0:1, 0:1], min_val=0, max_val=1)

                def aggregate(layer):
                    dve.wait_ge(y_copied, 1 + Q * (layer + 1))
                    for n in range(2):
                        dve.wait_ge(y_stored[n], 16 * SLOT_CH[n] * (layer + 1))
                    with dve.If(general == 0):
                        for h in range(2):
                            v.tensor_copy(stg[:, h * GT:(h + 1) * GT], srcT[:, h * GT:(h + 1) * GT]).then_inc(staged, 1)
                        with dve.Fori(0, NG // 2) as i:
                            for h in range(2):
                                k = i * 2 + h
                                for j in range(GT):
                                    n = h * GT + j
                                    t = i * (2 * GT) + n
                                    v.tensor_scalar(S[:, n * P:(n + 1) * P], iota[:, 0:P], dst_rel[:, bass.ds(t, 1)],
                                                    wT[:, bass.ds(t, 1)], ALU.is_equal, ALU.mult).then_inc(s_ready, 1)
                                b = dve.value_load(base_i[0:1, bass.ds(k, 1)], min_val=0, max_val=NP - P)
                                dve.wait_ge(summed, k + (NG * layer + 1))
                                v.tensor_copy(stg[:, h * GT:(h + 1) * GT],
                                              srcT[:, bass.ds(k * GT + 2 * GT, GT)]).then_inc(staged, 1)
                                dve.wait_ge(added, k + (NG * layer + 2))
                                a = acc[:, :, bass.ds(b, P)]
                                v.tensor_tensor(a, a, psum[:, 2 * h:2 * h + 2, 0:P], ALU.add).then_inc(added, 1)
                        dve.wait_ge(added, 2 + NG * (layer + 1))
                    with dve.Else():
                        with gen_chain.loop(ET, 1) as i:
                            v.tensor_copy(gstg[:, 0:1], srcT[:, bass.ds(i, 1)]).then_inc(gen_staged, 1)
                            gen_chain(v.tensor_scalar(dcol[:, :], offs[:, :], dstT[:, bass.ds(i, 1)], None, ALU.add))
                            for w in range(NW):
                                v.tensor_scalar(S[:, 0:WIN], iota[:, :], dcol[:, w:w + 1], wT[:, bass.ds(i, 1)],
                                                ALU.is_equal, ALU.mult).then_inc(gen_s, 1)
                                dve.wait_ge(gen_summed, i * NW + (ET * NW * layer + w + 1))
                                dve.wait_ge(gen_added, i * NW + (ET * NW * layer + w + 1))
                                a = acc[:, :, w * WIN:(w + 1) * WIN]
                                v.tensor_tensor(a, a, psum[:, 0:2, 0:WIN], ALU.add).then_inc(gen_added, 1)
                        dve.wait_ge(gen_added, 1 + ET * NW * (layer + 1))
                    v.memset(dscr[:, :], 0.0).then_inc(agg_done, 1)

                aggregate(0)

                with dve.Fori(0, NCH) as c:
                    for j in range(CH):
                        q = c * CH + j

                        def conv1(q, j):
                            dve.wait_ge(lin_done, q + 1)
                            dve.wait_ge(y_ready, q + (Q if j == 0 else Q - 1))
                            v.scalar_tensor_tensor(out=tmp[:, (j % 2) * D:(j % 2 + 1) * D], in0=bank(4 + j % 2, D),
                                                   scalar=dinv[:, bass.ds(q, 1)], in1=b1g[:, :],
                                                   op0=ALU.mult, op1=ALU.add).then_inc(lin_used, 1)

                        if j == 0:
                            conv1(q, 0)
                        if j + 1 < CH:
                            conv1(q + 1, j + 1)
                        copy_turned(1, q, j)

                aggregate(1)

                with dve.Fori(0, NCH) as c:
                    for j in range(CH):
                        q = c * CH + j
                        dve.wait_ge(lin_done, q + (Q + 1))
                        v.scalar_tensor_tensor(out=acc[:, :, bass.ds(q * P, P)],
                                               in0=bank(4 + j % 2, D).rearrange("p (c n) -> p c n", c=KC),
                                               scalar=dinv[:, bass.ds(q, 1)],
                                               in1=b2g[:, :].rearrange("p (c n) -> p c n", c=KC),
                                               op0=ALU.mult, op1=ALU.add).then_inc(lin_used, 1)
                dve.wait_ge(sum_done, 1)
                chain(v.tensor_scalar(mean_b[:, :], bank(6, D), 1.0 / N, None, ALU.mult))
                with dve.Fori(0, NCH) as c:
                    for k in range(KC):
                        a = acc[:, k, bass.ds(c * (CH * P), CH * P)].rearrange("p (t n) -> p t n", n=P)
                        v.tensor_tensor(a, a, mean_b[:, k * P:(k + 1) * P].unsqueeze(1).broadcast_to([P, CH, P]),
                                        ALU.subtract).then_inc(centred, 1)
                dve.wait_ge(sum_done, 2)
                v.tensor_scalar(sd_b[:, :], bank(7, D), 1.0 / N, BN_EPS, ALU.mult, ALU.add).then_inc(bn_var, 1)
                dve.wait_ge(bn_sd, 1)
                chain(v.reciprocal(scale_b[:, :], sd_b[:, :]))
                chain(v.tensor_tensor(scale_b[:, :], scale_b[:, :], gam[:, :], ALU.mult))

                for c in range(NCH):
                    for j in range(CH):
                        q = c * CH + j
                        a = acc[:, :, bass.ds(q * P, P)]
                        l = ln[:, (j % 2) * D:(j % 2 + 1) * D]
                        xt = X[:, bass.ds(q * D, D)]
                        chain(v.tensor_tensor(a, a, scale_b[:, :].rearrange("p (c n) -> p c n", c=KC), ALU.mult))
                        dve.wait_ge(lb_ready, q + 1)
                        chain(v.tensor_tensor(l.rearrange("p (c n) -> p c n", c=KC),
                                              l.rearrange("p (c n) -> p c n", c=KC), a, ALU.add))
                        chain(v.scalar_tensor_tensor(out=xt, in0=l, scalar=0.0, in1=xt, op0=ALU.max, op1=ALU.add))
                        v.bn_stats(stats[:, 6 * j:6 * j + 6], xt).then_inc(lb_used, 1)
                    chain(v.tensor_copy(dscr[:, :], zeros[:, 0:1]))
                    for j in range(CH):
                        v.bn_aggr(mv7[:, 2 * j:2 * j + 2], stats[:, 6 * j:6 * j + 6])
                    chain(v.tensor_copy(dscr[:, :], zeros[:, 0:1]))
                    chain(v.tensor_copy(mv[:, bass.ds(c * 2 * CH, 2 * CH)], mv7[:, :]))
                v.tensor_scalar(rstd[:, :], var, LN_EPS, None, ALU.add).then_inc(ln2_var, 1)
                dve.wait_ge(ln2_sd, 1)
                chain(v.reciprocal(mask[:, :], rstd[:, :]))
                chain(v.tensor_copy(rstd[:, :], mask[:, :]))
                v.scalar_tensor_tensor(out=nmr[:, :], in0=mean, scalar=-1.0, in1=rstd[:, :], op0=ALU.mult,
                                       op1=ALU.mult).then_inc(ln2_set, 1)
                with dve.Fori(0, NCH) as c:
                    for j in range(CH):
                        q = c * CH + j
                        dve.wait_ge(n_turned, q + 2)
                        v.tensor_copy(ln[:, (j % 2) * D:(j % 2 + 1) * D], bank(j % 2, D)).then_inc(n_copied, 1)

                def by_tile(ap):
                    return ap[:, :].rearrange("p (t e) -> p t e", e=NX)

                def per_tile(ap):
                    return ap[:, :].unsqueeze(2).broadcast_to([P, NT, NX])

                def per_expert(ap):
                    return ap[:, :].unsqueeze(1).broadcast_to([P, NT, NX])

                def tt(o, i0, i1, op):
                    chain(v.tensor_tensor(o, i0, i1, op))

                dve.wait_ge(logit_done, 1)
                tt(by_tile(prob), bank(2, T8).rearrange("p (t e) -> p t e", e=NX), per_expert(gb), ALU.add)
                chain(v.tensor_reduce(red[:, :], by_tile(prob), AX_X, ALU.max))
                v.tensor_tensor(by_tile(prob), by_tile(prob), per_tile(red), ALU.subtract).then_inc(lmax_set, 1)
                dve.wait_ge(exp_done, 1)
                chain(v.tensor_reduce(red[:, :], by_tile(prob), AX_X, ALU.add))
                chain(v.reciprocal(cw1[:, :], red[:, :]))
                tt(by_tile(prob), by_tile(prob), per_tile(cw1), ALU.mult)
                for sel, cw in ((sel1, cw1), (sel2, cw2)):
                    chain(v.tensor_reduce(cw[:, :], by_tile(prob), AX_X, ALU.max))
                    tt(by_tile(sA), by_tile(prob), per_tile(cw), ALU.is_equal)
                    tt(by_tile(sA), by_tile(sA), per_expert(rank8), ALU.mult)
                    chain(v.tensor_reduce(red[:, :], by_tile(sA), AX_X, ALU.max))
                    tt(by_tile(sel), by_tile(sA), per_tile(red), ALU.is_equal)
                    if sel is sel1:
                        chain(v.scalar_tensor_tensor(out=prob[:, :], in0=sel1[:, :], scalar=-2.0, in1=prob[:, :],
                                                     op0=ALU.mult, op1=ALU.add))
                chain(v.tensor_scalar(valid[:, NT - 1:NT], not_pad[:, 0:1], 1.0, None, ALU.add))
                tt(sA[:, :], sel1[:, :], sel2[:, :], ALU.add)
                v.tensor_tensor(by_tile(prob), by_tile(sA), per_tile(valid), ALU.mult).then_inc(member_set, 1)
                dve.wait_ge(rank_done, 1)
                chain(v.tensor_copy(sA[:, :], bank(4, T8)))
                now, then, shift = sA, sB, 1
                while shift < NT:
                    v.tensor_copy(then[:, 0:shift * NX], now[:, 0:shift * NX])
                    tt(then[:, shift * NX:T8], now[:, shift * NX:T8], now[:, 0:T8 - shift * NX], ALU.add)
                    now, then, shift = then, now, 2 * shift
                chain(v.tensor_scalar(cap[:, :], now[:, T8 - NX:T8], float(P - 1), None, ALU.add))
                chain(v.tensor_copy(cap_i[:, :], cap[:, :]))
                chain(v.tensor_scalar(cap_i[:, :], cap_i[:, :], -P, None, ALU.bitwise_and))
                chain(v.tensor_copy(endx[:, :], cap_i[:, :]))
                chain(v.tensor_copy(cap[:, :], endx[:, :]))
                for e in range(1, NX):
                    tt(endx[:, e:e + 1], endx[:, e - 1:e], cap[:, e:e + 1], ALU.add)
                tt(capx[:, :], endx[:, :], cap[:, :], ALU.subtract)
                tt(then[:, :], now[:, :], bank(4, T8), ALU.subtract)
                tt(then[:, :], then[:, :], bank(3, T8), ALU.add)
                tt(by_tile(then), by_tile(then), per_expert(capx), ALU.add)
                for k, sel in enumerate((sel1, sel2)):
                    tt(sel[:, :], sel[:, :], then[:, :], ALU.mult)
                    chain(v.tensor_reduce(pos[:, k * NT:(k + 1) * NT], by_tile(sel), AX_X, ALU.add))
                    tt(pos[:, k * NT:(k + 1) * NT], pos[:, k * NT:(k + 1) * NT], valid[:, :], ALU.mult)
                chain(v.tensor_copy(pos_g[:, :], pos[:, :]))
                for k in range(2):
                    a = pos[:, (k + 1) * NT - 1:(k + 1) * NT]
                    chain(v.tensor_scalar(dscr[:, :], trash[:, :], float(k * P), not_pad[:, 0:1], ALU.add, ALU.mult))
                    tt(a, a, dscr[:, :], ALU.subtract)
                chain(v.tensor_copy(pos_s[:, :], pos[:, :]))
                chain(v.tensor_scalar(texp_f[:, :], tile_at[:, :], endx[:, 0:1], None, ALU.is_ge))
                for e in range(1, NX - 1):
                    chain(v.scalar_tensor_tensor(out=texp_f[:, :], in0=tile_at[:, :], scalar=endx[:, e:e + 1],
                                                 in1=texp_f[:, :], op0=ALU.is_ge, op1=ALU.add))
                v.tensor_copy(texp_i[:, :], texp_f[:, :]).then_inc(b1_turned, 1)

                def stage_pos(table, c):
                    to = pstg[:, (c % 2) * 2 * CH:(c % 2 + 1) * 2 * CH].rearrange("p (t k) -> p t k", k=2)
                    at = table[:, :].rearrange("p (k t) -> p t k", k=2)
                    v.tensor_copy(to, at[:, CH * c:CH * (c + 1), :]).then_inc(pos_staged, 1)

                for c in range(NCH):
                    if c >= 2:
                        dve.wait_ge(scattered[c % 2], 16 * 2 * CH * (c // 2))
                    stage_pos(pos_s, c)

                def copy_x(j, slot):
                    dve.wait_ge(f_turned, j + 1)
                    v.tensor_copy(xsT[:, slot * D:(slot + 1) * D], bank(slot, D)).then_inc(f_copied, 1)

                def bias_out(j, slot, e, first):
                    dve.wait_ge(o_done, j + 2)
                    if not first:
                        dve.wait_ge(ys_out[slot], 16 * first_store(j, slot))
                    v.tensor_tensor(ys[:, slot * D:(slot + 1) * D], bank(4 + slot, D),
                                    b2e[:, bass.ds(e * D, D)], ALU.add).then_inc(ys_ready, 1)

                def expert_of(j):
                    return dve.value_load(texp_i[0:1, bass.ds(j, 1)], min_val=0, max_val=NX - 1)

                def first_store(j, slot):
                    return (j - slot) // 2 if isinstance(j, int) else None

                def stage_w1(j, slot, wait=True):
                    e = expert_of(j)
                    if wait:
                        dve.wait_ge(h_done, j - 1)
                    v.tensor_copy(w1s[:, slot * KC * H:(slot + 1) * KC * H],
                                  w1e[:, bass.ds(e * (KC * H), KC * H)]).then_inc(w1_staged, 1)

                dve.wait_ge(ld_exp, 16 * 2 * NX)
                for j in range(2):
                    copy_x(j, j)
                    stage_w1(j, j, False)
                for j in range(2):
                    copy_x(j + 2, j)
                    stage_w1(j + 2, j)
                    bias_out(j, j, expert_of(j), True)
                with dve.Fori(0, (FT - 4) // 2) as i:
                    for u in range(2):
                        e = expert_of(i * 2 + (u + 2))
                        copy_x(i * 2 + (u + 4), u)
                        stage_w1(i * 2 + (u + 4), u)
                        dve.wait_ge(o_done, i * 2 + (u + 4))
                        dve.wait_ge(ys_out[u], i * 16 + 16)
                        v.tensor_tensor(ys[:, u * D:(u + 1) * D], bank(4 + u, D),
                                        b2e[:, bass.ds(e * D, D)], ALU.add).then_inc(ys_ready, 1)
                for j in range(2 + (FT - 4) // 2 * 2, FT):
                    if j + 2 < FT:
                        copy_x(j + 2, j % 2)
                        stage_w1(j + 2, j % 2)
                    bias_out(j, j % 2, expert_of(j), False)

                for c in range(2):
                    dve.wait_ge(scattered[c], 16 * 2 * CH * SLOT_CH[c])
                    stage_pos(pos_g, c)
                for c in range(NCH):
                    dve.wait_ge(back[c % 2], 16 * 2 * CH * (c // 2 + 1))
                    if c + 2 < NCH:
                        stage_pos(pos_g, c + 2)
                    if c >= 2:
                        dve.wait_ge(o_out[c % 2], 16 * (c // 2))
                    for k in range(2):
                        for j in range(CH):
                            n, t = (c % 2) * CH + j, CH * c + j
                            ins = v.scalar_tensor_tensor(
                                out=OR[:, n * D:(n + 1) * D], in0=Y12[:, (2 * n + k) * D:(2 * n + k + 1) * D],
                                scalar=(cw1, cw2)[k][:, t:t + 1], op0=ALU.mult, op1=ALU.add,
                                in1=OR[:, n * D:(n + 1) * D] if k else X[:, t * D:(t + 1) * D])
                            if k:
                                ins.then_inc(o_ready, 1)
                        if k == 0:
                            chain(v.tensor_copy(dscr[:, :], zeros[:, 0:1]))

            @block.tensor
            def _(pe):
                m = nc.tensor
                pe.sem_inc(y_turned, 1)
                pe.sem_inc(sq_used, 1)
                pe.sem_inc(n_turned, 1)
                pe.sem_inc(o_done, 1)

                pe.wait_ge(consts_set, 1)
                for n, (rows, ready) in enumerate(((dst_rowf, 2), (w_row, 2), (src_rowf, 2))):
                    pe.wait_ge(edge_f, ready)
                    for b in range(RB):
                        ins = m.transpose(bank(2 * n, EC, 2)[:, b * P:(b + 1) * P], rows[:, b * P:(b + 1) * P], ident[:, :])
                    ins.then_inc(edges_turned, 1)
                pe.wait_ge(dstT_set, 1)
                m.matmul(bank(6, NG), ones[0:1, :], dstT[0:1, 0:ET:GT], start=True, stop=True).then_inc(base_bc, 1)

                m.matmul(bank(7, NT), ident[:, :], ones[:, 0:NT], start=True, stop=False, skip_group_check=True)
                with pe.Fori(0, ET // (2 * OH)) as i:
                    for h in range(2):
                        for j in range(OH):
                            n = h * OH + j
                            pe.wait_ge(hi_ready, i * (2 * OH) + (n + 1))
                            ins = m.matmul(bank(7, NT), LO[:, n * P:(n + 1) * P], HI[:, n * NT:(n + 1) * NT],
                                           start=False, stop=False, skip_group_check=True)
                        ins.then_inc(oh_free, 1)
                m.matmul(bank(7, NT), ident[:, :], zeros[:, 0:NT], start=False, stop=True,
                         skip_group_check=True).then_inc(deg_done, 1)
                pe.wait_ge(bad_set, 1)
                m.matmul(bank(6, 1), ones[:, :], bad[:, 3:4], start=True, stop=True).then_inc(bad_sum, 1)
                pe.wait_ge(ld_const, 16 * 10)
                pe.wait_ge(dve_chain, 2)
                m.transpose(bank(5, NX * HC), b1rows[0:NX * HC, 0:P], ident[0:NX * HC, 0:NX * HC]).then_inc(b1_turned, 1)

                def turn_rows(layer, q, n, j):
                    pe.wait_ge(y_ready, q + (Q * layer + 1))
                    pe.wait_ge(y_copied, prior(q, j) + Q * layer)
                    for k in range(KC):
                        ins = m.transpose(bank(j % 2, D)[:, k * P:(k + 1) * P],
                                          YR[:, n * D + k * P:n * D + (k + 1) * P], ident[:, :])
                    ins.then_inc(y_turned, 1)

                for c in range(NCH):
                    for j in range(CH):
                        turn_rows(0, CH * c + j, (c % 2) * CH + j, j)

                general = pe.value_load(flag_i[0:1, 0:1], min_val=0, max_val=1)

                def aggregate(layer):
                    pe.wait_ge(y_copied, 1 + Q * (layer + 1))
                    with pe.If(general == 0):
                        with pe.Fori(0, NG // 2) as i:
                            for h in range(2):
                                k = i * 2 + h
                                pe.wait_ge(added, k + (NG * layer + 1))
                                for j in range(GT):
                                    n = h * GT + j
                                    pe.wait_ge(s_ready, i * (2 * GT) + (ET * layer + n + 1))
                                    pe.wait_ge(gathered[n], i * 16 + (16 * (NG // 2) * layer + 16))
                                    for c in range(KC):
                                        ins = m.matmul(bank(2 * h + c, P), G[:, n * D + c * P:n * D + (c + 1) * P],
                                                       S[:, n * P:(n + 1) * P], start=(j == 0), stop=(j == GT - 1))
                                ins.then_inc(summed, 1)
                    with pe.Else():
                        with pe.Fori(0, ET) as i:
                            pe.wait_ge(gen_gathered, i * 16 + (16 * ET * layer + 16))
                            for w in range(NW):
                                pe.wait_ge(gen_s, i * NW + (ET * NW * layer + w + 1))
                                pe.wait_ge(gen_added, i * NW + (ET * NW * layer + w + 1))
                                for c in range(KC):
                                    ins = m.matmul(bank(c, WIN), G[:, c * P:(c + 1) * P], S[:, 0:WIN],
                                                   start=True, stop=True)
                                ins.then_inc(gen_summed, 1)
                    pe.wait_ge(agg_done, layer + 1)

                def linear(layer, q, j, W):
                    pe.wait_ge(lin_used, prior(q, j) + Q * layer)
                    for k in range(KC):
                        ins = m.matmul(bank(4 + j % 2, D), acc[:, k, bass.ds(q * P, P)], W[:, k * D:(k + 1) * D],
                                       start=(k == 0), stop=(k == KC - 1))
                    ins.then_inc(lin_done, 1)

                aggregate(0)
                for c in range(NCH):
                    for j in range(CH):
                        q = CH * c + j
                        if j == 0:
                            linear(0, q, 0, W1g)
                        if j + 1 < CH:
                            linear(0, q + 1, j + 1, W1g)
                        turn_rows(1, q, (c % 2) * CH + j, j)
                aggregate(1)

                acc_sum, acc_sq = bank(6, D), bank(7, D)

                def add_up(total, lhs, rhs, first=False, last=False):
                    return m.matmul(total.rearrange("p (c n) -> p c n", c=KC), lhs[:, :], rhs,
                                    start=first, stop=last, skip_group_check=True)

                z3 = zeros[:, :].rearrange("p (c n) -> p c n", c=KC)
                add_up(acc_sum, ones, z3, first=True)
                for c in range(NCH):
                    for j in range(CH):
                        q = c * CH + j
                        if j == 0:
                            linear(1, q, 0, W2g)
                        if j + 1 < CH:
                            linear(1, q + 1, j + 1, W2g)
                        pe.wait_ge(lin_used, q + (Q + 2))
                        add_up(acc_sum, ones, acc[:, :, bass.ds(q * P, P)])
                add_up(acc_sum, not_pad, acc[:, :, (NT - 1) * P:NT * P], last=True).then_inc(sum_done, 1)
                add_up(acc_sq, ones, z3, first=True)
                with pe.Fori(0, NCH) as c:
                    for j in range(CH):
                        q = c * CH + j
                        pe.wait_ge(sq_ready, q + 1)
                        add_up(acc_sq, ones, tmp[:, (j % 2) * D:(j % 2 + 1) * D].rearrange(
                            "p (c n) -> p c n", c=KC)).then_inc(sq_used, 1)
                add_up(acc_sq, not_pad, tmp[:, ((CH - 1) % 2) * D:((CH - 1) % 2 + 1) * D].rearrange(
                    "p (c n) -> p c n", c=KC), last=True).then_inc(sum_done, 1)

                def logits(q, j):
                    pe.wait_ge(n_copied, q + 2)
                    for k in range(KC):
                        ins = m.matmul(psum[:, 2, bass.ds(q * NX, NX)],
                                       ln[:, (j % 2) * D + k * P:(j % 2) * D + (k + 1) * P],
                                       gw[:, k * NX:(k + 1) * NX], start=(k == 0), stop=(k == KC - 1))
                    return ins

                with pe.Fori(0, NCH) as c:
                    for j in range(CH):
                        q = c * CH + j
                        pe.wait_ge(n_ready, q + 1)
                        pe.wait_ge(n_copied, prior(q, j))
                        for k in range(KC):
                            ins = m.transpose(bank(j % 2, D)[:, k * P:(k + 1) * P],
                                              tmp[:, (j % 2) * D + k * P:(j % 2) * D + (k + 1) * P], ident[:, :])
                        ins.then_inc(n_turned, 1)
                        if j > 0:
                            logits(q - 1, j - 1)
                    logits(c * CH + (CH - 1), CH - 1)
                m.matmul(bank(3, 8), ident[:, :], zeros[:, 0:8], start=True, stop=True).then_inc(logit_done, 1)

                pe.wait_ge(member_set, 1)
                m.matmul(bank(3, T8), before[:, :], prob[:, :], start=True, stop=True)
                m.matmul(bank(4, T8), ones[:, :], prob[:, :], start=True, stop=True).then_inc(rank_done, 1)

                pe.wait_ge(b1_turned, 2)
                pe.wait_ge(ld_exp, 16 * 2 * NX)

                def expert_of(j):
                    return pe.value_load(texp_i[0:1, bass.ds(j, 1)], min_val=0, max_val=NX - 1)

                def turn_x(j, s4, turn_of_slot):
                    pe.wait_ge(xs_in[s4], turn_of_slot)
                    for k in range(KC):
                        ins = m.transpose(bank(s4 % 2, D)[:, k * P:(k + 1) * P],
                                          xs[:, s4 * D + k * P:s4 * D + (k + 1) * P], ident[:, :])
                    ins.then_inc(f_turned, 1)

                def hidden(j, s):
                    pe.wait_ge(w1_staged, j + 1)
                    pe.wait_ge(f_copied, j + 1)
                    for c in range(HC):
                        for k in range(KC):
                            ins = m.matmul(psum[:, 2 + s, c * P:(c + 1) * P],
                                           w1s[:, s * KC * H + k * H + c * P:s * KC * H + k * H + (c + 1) * P],
                                           xsT[:, s * D + k * P:s * D + (k + 1) * P], start=(k == 0), stop=(k == KC - 1))
                    ins.then_inc(h_done, 1)

                def output(j, s, e):
                    pe.wait_ge(h_act, j + 1)
                    for c in range(HC):
                        ins = m.matmul(bank(4 + s, D), hT[:, s * H + c * P:s * H + (c + 1) * P],
                                       w2e[:, bass.ds(e * (HC * D) + c * D, D)], start=(c == 0), stop=(c == HC - 1))
                    ins.then_inc(o_done, 1)

                turn_x(0, 0, 16)
                turn_x(1, 1, 16)
                hidden(0, 0)

                def step(j, u, turn_of_slot, dynamic):
                    e = expert_of(j)
                    if dynamic or j + 2 < FT:
                        turn_x(j + 2, (u + 2) % 4, turn_of_slot)
                    if dynamic or j + 1 < FT:
                        hidden(j + 1, (u + 1) % 2)
                    if dynamic or j >= 2:
                        pe.wait_ge(ys_ready, j - 1)
                    output(j, u % 2, e)

                for j in range(4):
                    step(j, j, 16 * ((j + 2) // 4 + 1), False)
                loops = (FT - 6) // 4
                with pe.Fori(0, loops) as i:
                    for u in range(4):
                        step(i * 4 + (u + 4), u, i * 16 + 16 * ((u + 6) // 4 + 1), True)
                for j in range(4 + 4 * loops, FT):
                    step(j, j % 4, 16 * ((j + 2) // 4 + 1), False)


_INS = ['x', 'src', 'dst', 'edge_weight', 'L0_gnn_W1', 'L0_gnn_b1', 'L0_gnn_W2', 'L0_gnn_b2', 'L0_gnn_gamma',
        'L0_gnn_beta', 'L0_ffn_gate_w', 'L0_ffn_gate_b', 'L0_ffn_W1', 'L0_ffn_b1', 'L0_ffn_W2', 'L0_ffn_b2']
_OUTS = [((6250, 256), 'float32')]


def kernel(**inputs):
    import numpy as _np
    import concourse.bacc as _bacc
    from concourse import mybir as _mybir
    from concourse.bass_utils import run_bass_kernel_spmd as _run

    nc = _bacc.Bacc("TRN2", target_bir_lowering=False, num_devices=1)
    arrays, args = {}, []
    for name in _INS:
        a = _np.ascontiguousarray(inputs[name])
        arrays[f"in_{name}_dram"] = a
        args.append(nc.dram_tensor(f"in_{name}_dram", a.shape, _mybir.dt.from_np(a.dtype), kind="ExternalInput").ap())
    for i, (shape, dtype) in enumerate(_OUTS):
        dt = _mybir.dt.from_np(_np.dtype(dtype))
        args.append(nc.dram_tensor(f"out_{i}_dram", shape, dt, kind="ExternalOutput").ap())
    gnn_ffn(nc, *args)
    r = _run(nc, [arrays], core_ids=[0])
    return r.results[0]["out_0_dram"]
```

```python
from contextlib import ExitStack, contextmanager

import concourse.bass as bass
from concourse import mybir

F32 = mybir.dt.float32
I32 = mybir.dt.int32
BF16 = mybir.dt.bfloat16
ALU = mybir.AluOpType
ACT = mybir.ActivationFunctionType
AX_X = mybir.AxisListType.X

P = 128
CH = 7
GT = 14
OH = 8
WIN = 448
LN_EPS = 1e-05
BN_EPS = 1e-05


class Chain:

    def __init__(self, eng, sem):
        self.eng, self.sem, self.n, self.steps = eng, sem, 0, 0

    def __call__(self, ins):
        ins.then_inc(self.sem, 1)
        self.n, self.steps = self.n + 1, self.steps + 1
        self.eng.wait_ge(self.sem, self.n)

    @contextmanager
    def loop(self, count, steps):
        base, before = self.n, self.steps
        with self.eng.Fori(0, count) as i:
            self.n = i * steps + base
            yield i
            assert self.steps - before == steps, (self.steps - before, steps)
        self.n = base + steps * count


def gnn_ffn(nc, x, src, dst, edge_weight, g_W1, g_b1, g_W2, g_b2, g_gamma, g_beta,
            gate_w, gate_b, e_W1, e_b1, e_W2, e_b2, out):
    N, D = x.shape
    E = src.shape[0]
    NX, _, H = e_W1.shape
    KC = D // P
    HC = H // P
    NT = -(-N // P)
    TAIL = N - (NT - 1) * P
    NP = NT * P
    NCH = NT // CH
    ET = -(-E // (P * 2 * GT)) * 2 * GT
    NG = ET // GT
    RB = -(-(ET + 2 * GT) // P)
    EC = RB * P
    EFULL = E // P // P
    EROWS = E // P - EFULL * P
    EREST = E - (EFULL * P + EROWS) * P
    NW = NP // WIN
    FT = (2 * N + NX * (P - 1)) // P
    assert NT == NCH * CH and NP == NW * WIN and EFULL == RB - 1 and ET % (2 * OH) == 0 and KC == 2

    y_tab = [nc.dram_tensor(f"conv{n}_rows", (NP, D), F32, kind="Internal").ap() for n in range(2)]
    rows_x = nc.dram_tensor("rows_for_experts", (NP + P, D + 4), F32, kind="Internal").ap()

    with ExitStack() as ctx:
        def sb(name, cols, dt=F32):
            return ctx.enter_context(nc.sbuf_tensor(name, [P, cols], dt))

        def sem(name):
            return ctx.enter_context(nc.semaphore(name))

        X = sb("X", NT * D)
        ACC = sb("ACC", KC * NP)
        arena = sb("arena", NX * (KC * H + HC * D))
        acc = ACC[:, :].rearrange("p (c n) -> p c n", c=KC)

        edge_row = [arena[:, n * EC:(n + 1) * EC] for n in range(8)]
        src_row, dst_row, w_row = edge_row[0].bitcast(I32), edge_row[1].bitcast(I32), edge_row[2]
        src_rowf, dst_rowf = edge_row[3], edge_row[4]
        dst_lo, dst_hi, dint = edge_row[5], edge_row[6], edge_row[7].bitcast(I32)
        at = 2 * GT * D
        G = arena[:, 0:at]
        S = arena[:, at:at + 2 * GT * P]
        YR = arena[:, at:at + 2 * CH * D]
        Y0 = arena[:, 0:NT * D]
        at += 2 * GT * P
        LO = arena[:, at:at + 2 * OH * P]
        at += 2 * OH * P
        HI = arena[:, at:at + 2 * OH * NT]
        w1e = arena[:, 0:NX * KC * H]
        w2e = arena[:, NX * KC * H:NX * (KC * H + HC * D)]
        at = 0
        def early(cols, dt=F32):
            nonlocal at
            n = cols if dt == F32 else cols // 2
            at += n
            return ACC[:, at - n:at].bitcast(dt) if dt != F32 else ACC[:, at - n:at]
        lob = early(2 * GT * P, BF16)
        iota_b = early(GT * P, BF16)
        lo_b, second = early(EC, BF16), early(EC, BF16)
        w_part = [early(EC, BF16) for _ in range(3)]
        w_rest = early(EC)
        w_split = early(6 * ET, BF16)
        w_group = early(2 * 6 * GT, BF16)
        sums = w_rest[:, 0:6 * (NG + 2)]
        deg_cols, deg_rows, tile_is = early(2 * NG), early(P), early(NT)
        tile_col = early(2)
        tile_i = early(NG).bitcast(I32)
        tile_f = early(2 * NG)
        assert at <= KC * NP
        at = 0

        def late(cols, dt=F32):
            nonlocal at
            n = -(-cols // 2) if dt == BF16 else cols
            at += n
            a = ACC[:, at - n:at]
            return a if dt == F32 else a.bitcast(dt)[:, 0:cols]

        DX = D + 4
        T8 = NT * NX
        XN = late(2 * CH * DX)
        prob, sel1, sel2, sA, sB = [late(T8) for _ in range(5)]
        pos, texp_f, texp_i = late(2 * NT), late(FT), late(FT, I32)
        choice = late(4 * NT)
        tile_b = late(2 * NT, BF16)
        pos_i = prob[:, 0:2 * NT].bitcast(I32)
        pos_lo, pos_hi = [prob[:, n * NT:(n + 1) * NT].bitcast(BF16) for n in (2, 3)]
        slot_i = prob[:, 4 * NT:4 * NT + FT].bitcast(I32)
        ffn_at = at
        hot_lo = [late(CH * P, BF16) for _ in range(2)]
        hot_hi = [late(3 * CH * FT, BF16) for _ in range(2)]
        end = at
        at = ffn_at
        xs = late(4 * DX)
        xsT, hT, yb, ys = late(2 * D), late(2 * H), late(2 * D), late(4 * D)
        w1s = late(2 * KC * H)
        assert max(at, end) <= KC * NP

        edge_cols = sb("edge_cols", 4 * EC)
        srcT = edge_cols[:, 0:EC].bitcast(I32)
        dstT, wT, dst_rel = [edge_cols[:, n * EC:(n + 1) * EC] for n in (1, 2, 3)]
        ring = edge_cols[:, 0:2 * CH * D]
        assert 2 * CH * D <= 4 * EC
        base_f, base_i = sb("base_f", NG), sb("base_i", NG, I32)
        bad, flag_i = sb("bad", 4), sb("flag_i", 4, I32)
        stg = sb("stg", 2 * GT, I32)
        gstg = sb("gstg", 2, I32)
        iota = sb("iota", WIN)
        offs = sb("offs", NW)
        dcol = sb("dcol", NW)
        ident, before, ones, not_pad = [sb(n, P) for n in ("ident", "before", "ones", "not_pad")]
        zeros = sb("zeros", D)
        turns = sb("turns", 4)
        tmp = sb("tmp", 2 * D)
        rank8, place, spare = sb("rank8", NX), sb("place", 1), sb("spare", 1)
        iota7 = tmp[:, 0:CH * P // 2].bitcast(BF16)
        tile_at = sb("tile_at", FT)
        W1g, W2g = sb("W1g", KC * D), sb("W2g", KC * D)
        gw = sb("gw", KC * NX)
        b1g, b2g, gam, bet = [sb(n, D) for n in ("b1g", "b2g", "gam", "bet")]
        gb = sb("gb", NX)
        b2e = sb("b2e", NX * D)
        b1e = sb("b1e", NX * HC)
        deg, dinv, mask, rstd, nmr, sc, nb = [sb(n, NT) for n in ("deg", "dinv", "mask", "rstd", "nmr", "sc", "nb")]
        stats, mv = sb("stats", CH * 6), sb("mv", NT * 2)
        self_rows = ln = sb("ln", 2 * D)
        mean_b, scale_b = sb("mean_b", D), sb("scale_b", D)
        b1rows, sd_b = ln, mean_b
        red, cw1, cw2 = sb("red", NT), sb("cw1", NT), sb("cw2", NT)
        valid = sb("valid", NT)
        nmean, ssq = valid, red
        cap, capx, endx = sb("cap", NX), sb("capx", NX), sb("endx", NX)
        cap_i = sb("cap_i", NX, I32)
        pstg = sb("pstg", 8, I32)
        wab, wcol = sb("wab", 4), sb("wcol", 4)
        dscr = sb("dscr", 1)

        psum = ctx.enter_context(nc.psum_tensor("psum", [P, 8, 512], F32))

        def bank(b, cols, n=1):
            return psum[:, b:b + n, :].rearrange("p b f -> p (b f)")[:, 0:cols]

        ld_edges, ld_const, ld_exp = sem("ld_edges"), sem("ld_const"), sem("ld_exp")
        ld_x = [sem(f"ld_x{n}") for n in range(NCH)]
        r_pad, x_pad, zeros_set = sem("r_pad"), sem("x_pad"), sem("zeros_set")
        spare_zeroed = sem("spare_zeroed")
        consts_set, pool_chain = sem("consts_set"), sem("pool_chain")
        dve_chain, act_chain = sem("dve_chain"), sem("act_chain")
        edge_f, edges_turned = sem("edge_f"), sem("edges_turned")
        dstT_set, base_bc, bad_set, bad_sum, flag_set = [sem(n) for n in ("dstT_set", "base_bc", "bad_set", "bad_sum", "flag_set")]
        b1_turned = sem("b1_turned")
        oh_free, hi_ready, deg_done = sem("oh_free"), sem("hi_ready"), sem("deg_done")
        deg_var, deg_sd, sc_set = sem("deg_var"), sem("deg_sd"), sem("sc_set")
        lob_ready, deg_summed, deg_spread, deg_turned = [sem(n) for n in ("lob_ready", "deg_summed", "deg_spread", "deg_turned")]
        moments_set, y_ready, y0_act, y0_dve = [sem(n) for n in ("moments_set", "y_ready", "y0_act", "y0_dve")]
        acc_zero, self_turned, self_added = [sem(n) for n in ("acc_zero", "self_turned", "self_added")]
        self_in = [sem(f"self_in{n}") for n in range(2)]
        y_stored = [sem(f"y_stored{n}") for n in range(2)]
        staged, turn = sem("staged"), sem("turn")
        gathered = [sem(f"gathered{n}") for n in range(2 * GT)]
        s_ready, summed, added, agg_done = sem("s_ready"), sem("summed"), sem("added"), sem("agg_done")
        gen_staged, gen_turn, gen_gathered = sem("gen_staged"), sem("gen_turn"), sem("gen_gathered")
        sem_gen_chain, fast_chain = sem("gen_chain"), sem("fast_chain")
        ffn_turn, ffn_turn2 = sem("ffn_turn"), sem("ffn_turn2")
        gen_s, gen_summed, gen_added = sem("gen_s"), sem("gen_summed"), sem("gen_added")
        lin_done, lin_used = sem("lin_done"), sem("lin_used")
        z_added = sem("z_added")
        sum_done, centred, sq_ready, sq_used = sem("sum_done"), sem("centred"), sem("sq_ready"), sem("sq_used")
        bn_var, bn_sd, ln_ready, lb_ready, lb_used = [sem(n) for n in ("bn_var", "bn_sd", "ln_ready", "lb_ready", "lb_used")]
        ln2_var, ln2_sd, ln2_set = sem("ln2_var"), sem("ln2_sd"), sem("ln2_set")
        n_ready, n_turned, n_copied, logit_done = [sem(n) for n in ("n_ready", "n_turned", "n_copied", "logit_done")]
        lmax_set, exp_done = sem("lmax_set"), sem("exp_done")
        member_set, rank_done = sem("member_set"), sem("rank_done")
        xn_ready, choice_set, choice_in = sem("xn_ready"), sem("choice_set"), sem("choice_in")
        xn_stored = [sem(f"xn_stored{n}") for n in range(2)]
        total_set, iota7_set = sem("total_set"), sem("iota7_set")
        hot_ready, hot_used, slots_done = sem("hot_ready"), sem("hot_used"), sem("slots_done")
        g_staged, a_staged, row_weights, yb_ready, added_out = [
            sem(n) for n in ("g_staged", "a_staged", "row_weights", "yb_ready", "added_out")]
        xs_in = [sem(f"xs_in{n}") for n in range(4)]
        f_turned, f_copied, h_done, h_act, o_done, ys_ready = [sem(n) for n in ("f_turned", "f_copied", "h_done", "h_act", "o_done", "ys_ready")]
        w1_staged = sem("w1_staged")

        LOADS = 9
        OWN = (NT - 1) // 2
        STAGED = NG + 2
        Q = NT
        SLOT_CH = [(NCH + 1) // 2, NCH // 2]
        FFN_TURNS = (FT - 6) // 4
        Y_DVE = 4

        def four_by_four(eng, step):
            for j in range(4):
                step(j, j)
            with eng.Fori(1, FFN_TURNS) as i:
                for u in range(4):
                    step(i * 4 + u, u)
            for j in range(4 * FFN_TURNS, FT):
                step(j, j % 4)

        def slot(n):
            return ring[:, n * D:(n + 1) * D]

        def turned(j):
            return bank((0, 1, 3, 4, 5, 6, 7)[j], D)

        def prior(q, j):
            return q + 1 if j == 0 else q

        def rows_of(table, c, tiles=CH):
            return table[bass.ds(c * (CH * P), tiles * P), :].rearrange("(t p) d -> p t d", p=P)

        def tile3(ap, n=CH):
            return ap.rearrange("p (t d) -> p t d", t=n)

        with nc.Block() as block:

            @block.sync
            def _(sp):
                for a, r in ((src, src_row), (dst, dst_row), (edge_weight, w_row)):
                    sp.dma_start(r[:, 0:EFULL * P].rearrange("p (b e) -> p b e", b=EFULL),
                                 a[0:EFULL * P * P].rearrange("(b p e) -> p b e", p=P, e=P)).then_inc(ld_edges, 16)
                sp.wait_ge(r_pad, 3)
                for a, r in ((src, src_row), (dst, dst_row), (edge_weight, w_row)):
                    e0 = EFULL * P * P
                    sp.dma_start(r[0:EROWS, EFULL * P:EC],
                                 a[e0:e0 + EROWS * P].rearrange("(p e) -> p e", e=P)).then_inc(ld_edges, 16)
                    sp.dma_start(r[EROWS:EROWS + 1, EFULL * P:EFULL * P + EREST],
                                 a[e0 + EROWS * P:E].rearrange("(p e) -> p e", p=1)).then_inc(ld_edges, 16)
                for c in range(NCH):
                    if c < NCH - 1:
                        sp.dma_start(tile3(X[:, c * CH * D:(c + 1) * CH * D]), rows_of(x, c)).then_inc(ld_x[c], 16)
                    else:
                        sp.wait_ge(x_pad, 1)
                        t0 = (NT - 1) * D
                        sp.dma_start(tile3(X[:, c * CH * D:t0], CH - 1), rows_of(x, c, CH - 1)).then_inc(ld_x[c], 16)
                        sp.dma_start(X[0:TAIL, t0:t0 + D], x[(NT - 1) * P:N, :]).then_inc(ld_x[c], 16)
                sp.wait_ge(zeros_set, 1)
                sp.dma_start(rows_x[NP:NP + P, 0:D], zeros[:, :]).then_inc(spare_zeroed, 16)
                sp.dma_start(rows_x[NP:NP + P, D:DX], zeros[:, 0:DX - D]).then_inc(spare_zeroed, 16)

                def self_loads(layer):
                    for n in range(2):
                        sp.wait_ge(y_stored[n], 16 * SLOT_CH[n] * (layer + 1))
                    if layer:
                        sp.wait_ge(self_turned, 1 + Q * layer)
                    sp.dma_start(self_rows[:, 0:D], y_tab[layer][(NT - 1) * P:NP, :]).then_inc(self_in[0], 16)
                    with sp.Fori(0, (NT - 1) // 2) as i:
                        for h in range(2):
                            u = (h + 1) % 2
                            sp.wait_ge(self_turned, i * 2 + (Q * layer + h + 1))
                            sp.dma_start(self_rows[:, u * D:(u + 1) * D],
                                         y_tab[layer][bass.ds(i * (2 * P) + h * P, P), :]).then_inc(self_in[u], 16)

                for c in range(NCH):
                    sp.wait_ge(y0_dve, Y_DVE * (c + 1))
                    sp.wait_ge(y0_act, (CH - Y_DVE) * (c + 1))
                    sp.dma_start(rows_of(y_tab[0], c), tile3(Y0[:, c * CH * D:(c + 1) * CH * D])).then_inc(y_stored[c % 2], 16)
                self_loads(0)
                for c in range(NCH):
                    sp.wait_ge(y_ready, 1 + CH * (c + 1))
                    r0 = (c % 2) * CH * D
                    sp.dma_start(rows_of(y_tab[1], c), tile3(YR[:, r0:r0 + CH * D])).then_inc(y_stored[c % 2], 16)
                self_loads(1)

                sp.wait_ge(agg_done, 2)
                for e in range(NX):
                    sp.dma_start(w1e[:, e * KC * H:(e + 1) * KC * H].rearrange("p (c h) -> p c h", c=KC),
                                 e_W1[e].rearrange("(c p) h -> p c h", p=P)).then_inc(ld_exp, 16)
                    sp.dma_start(w2e[:, e * HC * D:(e + 1) * HC * D].rearrange("p (c d) -> p c d", c=HC),
                                 e_W2[e].rearrange("(c p) d -> p c d", p=P)).then_inc(ld_exp, 16)

                for c in range(NCH):
                    sp.wait_ge(lb_used, c + 1)
                    if c < NCH - 1:
                        sp.dma_start(rows_of(out, c), tile3(X[:, c * CH * D:(c + 1) * CH * D])).then_inc(total_set, 16)
                    else:
                        t0 = (NT - 1) * D
                        sp.dma_start(rows_of(out, c, CH - 1), tile3(X[:, c * CH * D:t0], CH - 1)).then_inc(total_set, 16)
                        sp.dma_start(out[(NT - 1) * P:N, :], X[0:TAIL, t0:t0 + D]).then_inc(total_set, 16)
                for c in range(NCH):
                    sp.wait_ge(xn_ready, CH * (c + 1))
                    sp.wait_ge(choice_in, c + 1)
                    r0 = (c % 2) * CH * DX
                    sp.dma_start(rows_of(rows_x, c), tile3(XN[:, r0:r0 + CH * DX])).then_inc(xn_stored[c % 2], 16)
                sp.wait_ge(added_out, 16 * FT)

            @block.gpsimd
            def _(pool):
                chain = Chain(pool, pool_chain)
                g = nc.gpsimd
                g.iota(iota[:, :], [[1, WIN]], base=0, channel_multiplier=0, allow_small_or_imprecise_dtypes=True)
                g.iota(offs[:, :], [[-WIN, NW]], base=0, channel_multiplier=0, allow_small_or_imprecise_dtypes=True)
                g.iota(rank8[:, :], [[-1, NX]], base=NX, channel_multiplier=0, allow_small_or_imprecise_dtypes=True)
                g.iota(place[:, :], [[0, 1]], base=0, channel_multiplier=1, allow_small_or_imprecise_dtypes=True)
                g.iota(spare[:, :], [[0, 1]], base=NP, channel_multiplier=1, allow_small_or_imprecise_dtypes=True)
                g.iota(tile_at[:, :], [[P, FT]], base=0, channel_multiplier=0, allow_small_or_imprecise_dtypes=True)
                g.memset(ident[:, :], 0.0)
                g.memset(before[:, :], 0.0)
                g.memset(ones[:, :], 1.0)
                g.iota(iota_b.rearrange("p (n t) -> p n t", t=GT), [[1, P], [0, GT]], base=0, channel_multiplier=0,
                       allow_small_or_imprecise_dtypes=True)
                chain(g.memset(not_pad[:, :], 0.0))
                g.affine_select(out=ident[:, :], in_=ident[:, :], compare_op=ALU.not_equal, fill=1.0, base=0,
                                pattern=[[-1, P]], channel_multiplier=1)
                g.affine_select(out=before[:, :], in_=before[:, :], compare_op=ALU.is_ge, fill=1.0, base=0,
                                pattern=[[-1, P]], channel_multiplier=1)
                g.affine_select(out=not_pad[:, :], in_=not_pad[:, :], compare_op=ALU.is_gt, fill=-1.0, base=TAIL,
                                pattern=[[0, P]], channel_multiplier=-1).then_inc(consts_set, 1)

                def take_turn(sem_turn, n, at=0):
                    pool.wait_ge(sem_turn, n)
                    g.tensor_tensor(turns[:, at:at + 1], zeros[:, 0:1], zeros[:, 1:2], ALU.add).then_inc(sem_turn, 1)

                pool.sem_inc(turn, 1)
                pool.sem_inc(gen_turn, 1)
                pool.wait_ge(zeros_set, 1)
                pool.wait_ge(flag_set, 1)
                general = pool.value_load(flag_i[0:1, 0:1], min_val=0, max_val=1)
                pool.wait_ge(sc_set, 1)
                g.memset(ACC[:, :], 0.0).then_inc(acc_zero, 1)
                for layer in range(2):
                    if layer == 1:
                        for c in range(NCH):
                            pool.wait_ge(lin_done, CH * (c + 1))
                            g.memset(acc[:, :, c * CH * P:(c + 1) * CH * P], 0.0).then_inc(acc_zero, 1)
                    for n in range(2):
                        pool.wait_ge(y_stored[n], 16 * SLOT_CH[n] * (layer + 1))
                    with pool.If(general == 0):
                        with pool.Fori(0, NG // 2) as i:
                            for h in range(2):
                                pool.wait_ge(staged, i * 2 + (STAGED * layer + h + 1))
                                take_turn(turn, i * 2 + (NG * layer + h + 1))
                                for j in range(GT):
                                    n = h * GT + j
                                    pool.indirect_dma_start(
                                        G[:, n * D:(n + 1) * D], None, y_tab[layer],
                                        bass.IndirectOffsetOnAxis(stg[:, n:n + 1], 0)).then_inc(gathered[n], 16)
                    with pool.Else():
                        with pool.Fori(0, ET) as i:
                            pool.wait_ge(gen_staged, i + (ET * layer + 1))
                            take_turn(gen_turn, i + (ET * layer + 1))
                            pool.indirect_dma_start(
                                G[:, 0:D], None, y_tab[layer],
                                bass.IndirectOffsetOnAxis(gstg[:, 0:1], 0)).then_inc(gen_gathered, 16)

                pool.wait_ge(agg_done, 2)
                g.memset(tmp[:, :], 0.0).then_inc(z_added, 1)
                with pool.Fori(0, NCH) as c:
                    for j in range(CH):
                        q = c * CH + j
                        pool.wait_ge(lin_used, q + (Q + 2))
                        pool.wait_ge(z_added, prior(q, j))
                        z = tmp[:, (j % 2) * D:(j % 2 + 1) * D].rearrange("p (c n) -> p c n", c=KC)
                        g.tensor_tensor(z, z, acc[:, :, bass.ds(q * P, P)], ALU.add).then_inc(z_added, 1)

                for c in range(NCH):
                    for j in range(CH):
                        pool.wait_ge(ln_ready, c * CH + j + 1)
                        a = slot(c % 2 * CH + j)
                        g.tensor_tensor(a, a, bet[:, :], ALU.add).then_inc(lb_ready, 1)

                pool.wait_ge(logit_done, 1)
                g.iota(iota7.rearrange("p (n t) -> p n t", t=CH), [[1, P], [0, CH]], base=0, channel_multiplier=0,
                       allow_small_or_imprecise_dtypes=True)
                g.iota(tile_b.rearrange("p (k t) -> p k t", k=2), [[0, 2], [1, NT]], base=0, channel_multiplier=0,
                       allow_small_or_imprecise_dtypes=True).then_inc(iota7_set, 1)
                pool.wait_ge(choice_set, 1)
                for c in range(NCH):
                    if c >= 2:
                        pool.wait_ge(xn_stored[c % 2], 16 * (c // 2))
                    g.tensor_copy(tile3(XN[:, (c % 2) * CH * DX:(c % 2 + 1) * CH * DX])[:, :, D:DX],
                                  choice[:, 4 * CH * c:4 * CH * (c + 1)].rearrange("p (t k) -> p t k", k=4)
                                  ).then_inc(choice_in, 1)

                for n in range(2):
                    pool.wait_ge(xn_stored[n], 16 * SLOT_CH[n])
                pool.wait_ge(spare_zeroed, 32)
                pool.wait_ge(total_set, 16 * (NCH + 1))

                def gather(n, u):
                    pool.wait_ge(g_staged, n + 1)
                    take_turn(ffn_turn, n + 1, 1)
                    pool.indirect_dma_start(xs[:, u * DX:(u + 1) * DX], None, rows_x,
                                            bass.IndirectOffsetOnAxis(pstg[:, u:u + 1], 0)).then_inc(xs_in[u], 16)

                def scatter_add(n, u):
                    pool.wait_ge(a_staged, n + 1)
                    pool.wait_ge(ys_ready, n + 1)
                    if not isinstance(n, int) or n:
                        pool.wait_ge(added_out, n * 16)
                    take_turn(ffn_turn2, n + 1, 2)
                    pool.indirect_dma_start(out, bass.IndirectOffsetOnAxis(pstg[:, 4 + u:5 + u], 0),
                                            ys[:, u * D:(u + 1) * D], None, bounds_check=N - 1, oob_is_err=False,
                                            compute_op=ALU.add).then_inc(added_out, 16)

                pool.sem_inc(ffn_turn, 1)
                pool.sem_inc(ffn_turn2, 1)
                for n in range(4):
                    gather(n, n)

                def ffn_step(j, u):
                    if not isinstance(j, int) or j + 4 < FT:
                        gather(j + 4, u)
                    scatter_add(j, u)

                four_by_four(pool, ffn_step)

            @block.scalar
            def _(act):
                chain = Chain(act, act_chain)
                a = nc.scalar
                act.dma_start(W1g[:, :].rearrange("p (c d) -> p c d", c=KC),
                              g_W1.rearrange("(c p) d -> p c d", p=P)).then_inc(ld_const, 16)
                act.dma_start(W2g[:, :].rearrange("p (c d) -> p c d", c=KC),
                              g_W2.rearrange("(c p) d -> p c d", p=P)).then_inc(ld_const, 16)
                act.dma_start(gw[:, :].rearrange("p (c e) -> p c e", c=KC),
                              gate_w.rearrange("(c p) e -> p c e", p=P)).then_inc(ld_const, 16)
                for to, row in ((b1g, g_b1), (b2g, g_b2), (gam, g_gamma), (bet, g_beta), (gb, gate_b)):
                    act.dma_start(to[:, :], row.partition_broadcast(P)).then_inc(ld_const, 16)
                act.dma_start(b2e[:, :], e_b2.rearrange("e d -> (e d)").partition_broadcast(P)).then_inc(ld_const, 16)
                act.dma_start(b1rows[0:NX * HC, 0:P],
                              e_b1.rearrange("e (c p) -> (e c) p", p=P)).then_inc(ld_const, 16)

                for c in range(NCH):
                    act.wait_ge(ld_x[c], 32 if c == NCH - 1 else 16)
                    tiles = range(CH * c, CH * (c + 1))
                    for t in tiles:
                        chain(a.activation(tmp[:, 0:D], X[:, t * D:(t + 1) * D], ACT.Identity, scale=-1.0 / D,
                                           accum_out=nmean[:, t:t + 1]))
                    for t in tiles:
                        chain(a.activation(tmp[:, 0:D], X[:, t * D:(t + 1) * D], ACT.Square, bias=nmean[:, t:t + 1],
                                           accum_out=ssq[:, t:t + 1]))
                a.activation(tmp[:, D:D + 1], tmp[:, 0:1], ACT.Identity).then_inc(moments_set, 1)

                act.wait_ge(deg_var, 1)
                a.activation(rstd[:, :], rstd[:, :], ACT.Sqrt).then_inc(deg_sd, 1)
                act.wait_ge(deg_var, 2)
                a.activation(deg[:, :], deg[:, :], ACT.Sqrt).then_inc(deg_sd, 1)

                act.wait_ge(sc_set, 1)
                for c in range(NCH):
                    for j in range(Y_DVE, CH):
                        t = CH * c + j
                        a.activation(Y0[:, t * D:(t + 1) * D], X[:, t * D:(t + 1) * D], ACT.Identity,
                                     bias=nb[:, t:t + 1], scale=sc[:, t:t + 1]).then_inc(y0_act, 1)

                act.sem_inc(y_ready, 1)
                for c in range(NCH):
                    for j in range(CH):
                        n, t = (c % 2) * CH + j, CH * c + j
                        if c >= 2 and j == 0:
                            act.wait_ge(y_stored[c % 2], 16 * (SLOT_CH[c % 2] + c // 2))
                        act.wait_ge(lin_used, 1 + t + 1)
                        a.activation(YR[:, n * D:(n + 1) * D], tmp[:, (j % 2) * D:(j % 2 + 1) * D], ACT.Relu,
                                     scale=dinv[:, t:t + 1]).then_inc(y_ready, 1)

                with act.Fori(0, NCH) as c:
                    act.wait_ge(centred, c * 2 + 2)
                    for j in range(CH):
                        q = c * CH + j
                        act.wait_ge(sq_used, q + 1)
                        a.activation(slot(j).rearrange("p (c n) -> p c n", c=KC),
                                     acc[:, :, bass.ds(q * P, P)], ACT.Square).then_inc(sq_ready, 1)
                act.wait_ge(bn_var, 1)
                a.activation(sd_b[:, :], sd_b[:, :], ACT.Sqrt).then_inc(bn_sd, 1)

                def norm_x(c):
                    if c >= 2:
                        act.wait_ge(lb_used, c - 1)
                    for j in range(CH):
                        q = c * CH + j
                        a.activation(slot(c % 2 * CH + j), X[:, q * D:(q + 1) * D], ACT.Identity,
                                     bias=nmr[:, q:q + 1], scale=rstd[:, q:q + 1]).then_inc(ln_ready, 1)

                def copy_turned(c):
                    for j in range(CH):
                        q = c * CH + j
                        act.wait_ge(n_turned, q + 1)
                        a.activation(acc[:, :, q * P:(q + 1) * P], turned(j).rearrange("p (c n) -> p c n", c=KC),
                                     ACT.Copy).then_inc(n_copied, 1)

                norm_x(0)
                norm_x(1)
                for c in range(NCH):
                    tiles = slice(c * CH, (c + 1) * CH)
                    act.wait_ge(ln2_var, c + 1)
                    a.activation(rstd[:, tiles], rstd[:, tiles], ACT.Sqrt).then_inc(ln2_sd, 1)
                    if c:
                        copy_turned(c - 1)
                    act.wait_ge(ln2_set, c + 1)
                    for q in range(c * CH, (c + 1) * CH):
                        a.activation(acc[:, :, q * P:(q + 1) * P],
                                     X[:, q * D:(q + 1) * D].rearrange("p (c n) -> p c n", c=KC), ACT.Identity,
                                     bias=nmr[:, q:q + 1], scale=rstd[:, q:q + 1]).then_inc(n_ready, 1)
                    if c + 2 < NCH:
                        norm_x(c + 2)
                copy_turned(NCH - 1)
                act.wait_ge(lmax_set, 1)
                a.activation(prob[:, :], prob[:, :], ACT.Exp).then_inc(exp_done, 1)

                for c in range(NCH):
                    if c >= 2:
                        act.wait_ge(xn_stored[c % 2], 16 * (c // 2))
                    for j in range(CH):
                        n, t = (c % 2) * CH + j, CH * c + j
                        a.activation(XN[:, n * DX:n * DX + D], X[:, t * D:(t + 1) * D], ACT.Identity,
                                     bias=nmr[:, t:t + 1], scale=rstd[:, t:t + 1]).then_inc(xn_ready, 1)

                def gelu(j, slot):
                    e = act.value_load(texp_i[0:1, bass.ds(j, 1)], min_val=0, max_val=NX - 1)
                    act.wait_ge(h_done, j + 1)
                    if not isinstance(j, int) or j >= 1:
                        act.wait_ge(o_done, j)
                    for c in range(HC):
                        ins = a.activation(hT[:, slot * H + c * P:slot * H + (c + 1) * P],
                                           psum[:, 2 + slot, c * P:(c + 1) * P], ACT.Gelu,
                                           bias=b1e[:, bass.ds(e * HC + c, 1)])
                    ins.then_inc(h_act, 1)

                def ffn_step(j, u):
                    if not isinstance(j, int) or j + 1 < FT:
                        gelu(j + 1, (u + 1) % 2)
                    act.wait_ge(yb_ready, j + 1)
                    if not isinstance(j, int) or j >= 4:
                        act.wait_ge(added_out, (j - 3) * 16)
                    a.activation(ys[:, u * D:(u + 1) * D], yb[:, (u % 2) * D:(u % 2 + 1) * D], ACT.Copy,
                                 scale=wcol[:, u:u + 1]).then_inc(ys_ready, 1)

                act.wait_ge(b1_turned, 2)
                gelu(0, 0)
                four_by_four(act, ffn_step)

            @block.vector
            def _(dve):
                chain, gen_chain, chain_fast = [Chain(dve, x) for x in (dve_chain, sem_gen_chain, fast_chain)]
                v = nc.vector
                last0 = EFULL * P
                v.memset(src_row[:, last0:EC], 0).then_inc(r_pad, 1)
                v.memset(dst_row[:, last0:EC], N - 1).then_inc(r_pad, 1)
                v.memset(w_row[:, last0:EC], 0.0).then_inc(r_pad, 1)
                v.memset(X[:, (NT - 1) * D:NT * D], 0.0).then_inc(x_pad, 1)
                v.memset(zeros[:, :], 0.0).then_inc(zeros_set, 1)
                dve.sem_inc(oh_free, 2)
                dve.sem_inc(self_added, 2)
                dve.sem_inc(added, 2)
                dve.sem_inc(gen_added, 1)
                dve.sem_inc(lin_used, 1)

                dve.wait_ge(ld_edges, 16 * LOADS)
                v.tensor_copy(dst_rowf, dst_row).then_inc(edge_f, 1)
                v.tensor_copy(src_rowf, src_row).then_inc(edge_f, 1)
                dve.wait_ge(edges_turned, 1)
                v.tensor_copy(dstT[:, :], bank(0, EC, 2)).then_inc(dstT_set, 1)
                chain(v.tensor_copy(dint[:, :], bank(0, EC, 2)))

                dve.wait_ge(base_bc, 1)
                chain(v.tensor_scalar(base_f[:, :], bank(6, NG), float(NP - P), None, ALU.min))
                chain(v.tensor_copy(base_i[:, :], base_f[:, :]))
                chain(v.tensor_tensor(dst_rel[:, 0:ET].rearrange("p (g t) -> p g t", t=GT),
                                      dstT[:, 0:ET].rearrange("p (g t) -> p g t", t=GT),
                                      base_f[:, :].unsqueeze(2).broadcast_to([P, NG, GT]), ALU.subtract))
                v.tensor_reduce(bad[:, 0:1], dst_rel[:, 0:ET], AX_X, ALU.max)
                chain(v.tensor_reduce(bad[:, 1:2], dst_rel[:, 0:ET], AX_X, ALU.min))
                chain(v.tensor_scalar(bad[:, 2:3], bad[:, 0:1], float(P - 1), None, ALU.is_gt))
                v.tensor_scalar(bad[:, 3:4], bad[:, 1:2], 0.0, bad[:, 2:3], ALU.is_lt, ALU.add).then_inc(bad_set, 1)
                dve.wait_ge(bad_sum, 1)
                chain(v.tensor_scalar(bad[:, 0:1], bank(6, 1), 0.5, None, ALU.is_gt))
                v.tensor_copy(flag_i[:, 0:1], bad[:, 0:1]).then_inc(flag_set, 1)

                v.tensor_scalar(dst_lo[:, :].bitcast(I32), dint[:, :], P - 1, None, ALU.bitwise_and)
                v.tensor_scalar(dst_hi[:, :].bitcast(I32), dint[:, :], P.bit_length() - 1, None, ALU.logical_shift_right)
                chain(v.tensor_scalar(tile_i[:, :], base_i[:, :], P.bit_length() - 1, None, ALU.logical_shift_right))
                tiles2 = tile_f[:, :].rearrange("p (g s) -> p g s", s=2)
                v.tensor_copy(tiles2[:, :, 0], tile_i[:, :])
                v.tensor_copy(lo_b, dst_lo[:, :].bitcast(I32))
                chain(v.tensor_copy(dint[:, :].bitcast(F32), dst_hi[:, :].bitcast(I32)))
                v.tensor_scalar(tiles2[:, :, 1], tiles2[:, :, 0], 1.0, None, ALU.add)
                v.tensor_tensor(second[:, 0:ET].rearrange("p (g t) -> p g t", t=GT),
                                dint[:, 0:ET].bitcast(F32).rearrange("p (g t) -> p g t", t=GT),
                                tiles2[:, :, 0:1].broadcast_to([P, NG, GT]), ALU.subtract)
                dve.wait_ge(edges_turned, 2)
                chain(v.tensor_copy(wT[:, :], bank(2, EC, 2)))
                chain(v.tensor_copy(w_part[0], wT[:, :]))
                chain(v.tensor_tensor(w_rest, wT[:, :], w_part[0], ALU.subtract))
                chain(v.tensor_copy(w_part[1], w_rest))
                chain(v.tensor_tensor(w_rest, w_rest, w_part[1], ALU.subtract))
                chain(v.tensor_copy(w_part[2], w_rest))
                split = w_split.rearrange("p (t s k) -> p t s k", s=2, k=3)
                for k in range(3):
                    v.tensor_tensor(split[:, :, 1, k], w_part[k][:, 0:ET], second[:, 0:ET], ALU.mult)
                chain(v.tensor_copy(dscr[:, :], zeros[:, 0:1]))
                for k in range(3):
                    v.tensor_tensor(split[:, :, 0, k], w_part[k][:, 0:ET], split[:, :, 1, k], ALU.subtract)
                chain(v.tensor_copy(dscr[:, :], zeros[:, 0:1]))

                general = dve.value_load(flag_i[0:1, 0:1], min_val=0, max_val=1)
                dve.wait_ge(consts_set, 1)
                with dve.If(general == 0):
                    with dve.Fori(0, NG // 2) as i:
                        for h in range(2):
                            dve.wait_ge(oh_free, i * 2 + (h + 1))
                            v.tensor_copy(sums[:, bass.ds(i * 12 + h * 6, 6)], bank(2 + h, 6))
                            v.tensor_copy(w_group[:, h * 6 * GT:(h + 1) * 6 * GT],
                                          w_split[:, bass.ds(i * (12 * GT) + h * 6 * GT, 6 * GT)])
                            v.tensor_tensor(lob[:, h * GT * P:(h + 1) * GT * P].rearrange("p (n t) -> p n t", t=GT),
                                            iota_b.rearrange("p (n t) -> p n t", t=GT),
                                            lo_b[:, bass.ds(i * (2 * GT) + h * GT, GT)].unsqueeze(1).broadcast_to([P, P, GT]),
                                            ALU.is_equal).then_inc(lob_ready, 1)
                    dve.wait_ge(oh_free, 2 + NG)
                    for h in range(2):
                        ins = v.tensor_copy(sums[:, 6 * (NG + h):6 * (NG + h + 1)], bank(2 + h, 6))
                    chain_fast(ins)
                    v.tensor_reduce(deg_cols, sums[:, 12:6 * (NG + 2)].rearrange("p (g k) -> p g k", k=3), AX_X,
                                    ALU.add).then_inc(deg_summed, 1)
                    dve.wait_ge(deg_turned, 1)
                    v.tensor_copy(deg_rows[0:2 * NG, :], bank(0, P)[0:2 * NG, :])
                    chain_fast(v.tensor_copy(tile_col[0:2 * NG, 0:1], bank(1, P)[0:2 * NG, 0:1]))
                    v.tensor_scalar(tile_is[0:2 * NG, :], iota[0:2 * NG, 0:NT], tile_col[0:2 * NG, 0:1], None,
                                    ALU.is_equal).then_inc(deg_spread, 1)
                with dve.Else():
                    gen_chain(v.tensor_copy(dst_lo[:, :], dst_lo[:, :].bitcast(I32)))
                    gen_chain(v.tensor_copy(dst_hi[:, :], dint[:, :].bitcast(F32)))
                    with dve.Fori(0, ET // (2 * OH)) as i:
                        for h in range(2):
                            dve.wait_ge(oh_free, i * 2 + (h + 1))
                            for j in range(OH):
                                n = h * OH + j
                                t = i * (2 * OH) + n
                                v.tensor_scalar(LO[:, n * P:(n + 1) * P], iota[:, 0:P], dst_lo[:, bass.ds(t, 1)], None,
                                                ALU.is_equal)
                                v.tensor_scalar(HI[:, n * NT:(n + 1) * NT], iota[:, 0:NT], dst_hi[:, bass.ds(t, 1)],
                                                wT[:, bass.ds(t, 1)], ALU.is_equal, ALU.mult).then_inc(hi_ready, 1)
                dve.wait_ge(edges_turned, 3)
                v.tensor_copy(srcT[:, :], bank(4, EC, 2))
                dve.wait_ge(b1_turned, 1)
                v.tensor_copy(b1e[:, :], bank(6, NX * HC)[:, 0:NX * HC])

                mean, var = [mv[:, :].rearrange("p (t k) -> p t k", k=2)[:, :, k] for k in range(2)]
                dve.wait_ge(moments_set, 1)
                v.tensor_scalar(rstd[:, :], ssq[:, :], 1.0 / D, LN_EPS, ALU.mult, ALU.add).then_inc(deg_var, 1)
                dve.wait_ge(deg_done, 1)
                chain(v.tensor_scalar(deg[:, :], bank(7, NT), 1.0, None, ALU.add))
                chain(v.tensor_scalar(mask[:, :], deg[:, :], 0.0, None, ALU.is_gt))
                v.tensor_scalar(deg[:, :], deg[:, :], 1e-30, None, ALU.max).then_inc(deg_var, 1)
                dve.wait_ge(deg_sd, 2)
                v.reciprocal(nb[:, :], rstd[:, :])
                chain(v.reciprocal(dinv[:, :], deg[:, :]))
                v.tensor_copy(rstd[:, :], nb[:, :])
                chain(v.tensor_tensor(dinv[:, :], dinv[:, :], mask[:, :], ALU.mult))
                v.tensor_tensor(nmr[:, :], nmean[:, :], rstd[:, :], ALU.mult)
                chain(v.tensor_tensor(sc[:, :], rstd[:, :], dinv[:, :], ALU.mult))
                v.tensor_tensor(nb[:, :], nmr[:, :], dinv[:, :], ALU.mult).then_inc(sc_set, 1)
                dve.wait_ge(sc_set, 1)
                for c in range(NCH):
                    for j in range(Y_DVE):
                        t = CH * c + j
                        v.tensor_scalar(Y0[:, t * D:(t + 1) * D], X[:, t * D:(t + 1) * D], sc[:, t:t + 1],
                                        nb[:, t:t + 1], ALU.mult, ALU.add).then_inc(y0_dve, 1)

                def add_self(layer, n, t, u):
                    dve.wait_ge(self_turned, n + (1 + Q * layer + 1))
                    a = acc[:, :, bass.ds(t * P, P)]
                    v.tensor_tensor(a, a, bank(4 + u, D).rearrange("p (c n) -> p c n", c=KC),
                                    ALU.add).then_inc(self_added, 1)

                def aggregate(layer):
                    dve.wait_ge(acc_zero, 1 + NCH * layer)
                    for n in range(2):
                        dve.wait_ge(y_stored[n], 16 * SLOT_CH[n] * (layer + 1))
                    add_self(layer, 0, NT - 1, 0)
                    with dve.If(general == 0):
                        for h in range(2):
                            v.tensor_copy(stg[:, h * GT:(h + 1) * GT], srcT[:, h * GT:(h + 1) * GT]).then_inc(staged, 1)
                        def group(i, h, own):
                            k = i * 2 + h
                            for j in range(GT):
                                n = h * GT + j
                                t = i * (2 * GT) + n
                                v.tensor_scalar(S[:, n * P:(n + 1) * P], iota[:, 0:P], dst_rel[:, bass.ds(t, 1)],
                                                wT[:, bass.ds(t, 1)], ALU.is_equal, ALU.mult).then_inc(s_ready, 1)
                            b = dve.value_load(base_i[0:1, bass.ds(k, 1)], min_val=0, max_val=NP - P)
                            dve.wait_ge(added, k + (NG * layer + 2))
                            if own:
                                add_self(layer, k + 1, k, (h + 1) % 2)
                            dve.wait_ge(summed, k + (NG * layer + 1))
                            v.tensor_copy(stg[:, h * GT:(h + 1) * GT],
                                          srcT[:, bass.ds(k * GT + 2 * GT, GT)]).then_inc(staged, 1)
                            if own:
                                dve.wait_ge(self_added, k + (Q * layer + 4))
                            a = acc[:, :, bass.ds(b, P)]
                            v.tensor_tensor(a, a, psum[:, 2 * h:2 * h + 2, 0:P], ALU.add).then_inc(added, 1)

                        dve.wait_ge(self_added, Q * layer + 3)
                        with dve.Fori(0, OWN) as i:
                            for h in range(2):
                                group(i, h, True)
                        with dve.Fori(OWN, NG // 2) as i:
                            for h in range(2):
                                group(i, h, False)
                        dve.wait_ge(added, 2 + NG * (layer + 1))
                    with dve.Else():
                        with dve.Fori(0, OWN) as i:
                            for h in range(2):
                                add_self(layer, i * 2 + (h + 1), i * 2 + h, (h + 1) % 2)
                        dve.wait_ge(self_added, 2 + Q * (layer + 1))
                        with gen_chain.loop(ET, 1) as i:
                            v.tensor_copy(gstg[:, 0:1], srcT[:, bass.ds(i, 1)]).then_inc(gen_staged, 1)
                            gen_chain(v.tensor_scalar(dcol[:, :], offs[:, :], dstT[:, bass.ds(i, 1)], None, ALU.add))
                            for w in range(NW):
                                v.tensor_scalar(S[:, 0:WIN], iota[:, :], dcol[:, w:w + 1], wT[:, bass.ds(i, 1)],
                                                ALU.is_equal, ALU.mult).then_inc(gen_s, 1)
                                dve.wait_ge(gen_summed, i * NW + (ET * NW * layer + w + 1))
                                dve.wait_ge(gen_added, i * NW + (ET * NW * layer + w + 1))
                                a = acc[:, :, w * WIN:(w + 1) * WIN]
                                v.tensor_tensor(a, a, psum[:, 0:2, 0:WIN], ALU.add).then_inc(gen_added, 1)
                        dve.wait_ge(gen_added, 1 + ET * NW * (layer + 1))
                    v.memset(dscr[:, :], 0.0).then_inc(agg_done, 1)

                aggregate(0)

                with dve.Fori(0, NCH) as c:
                    for j in range(CH):
                        q = c * CH + j
                        dve.wait_ge(lin_done, q + 1)
                        dve.wait_ge(y_ready, prior(q, j))
                        v.scalar_tensor_tensor(out=tmp[:, (j % 2) * D:(j % 2 + 1) * D], in0=bank(6 + j % 2, D),
                                               scalar=dinv[:, bass.ds(q, 1)], in1=b1g[:, :],
                                               op0=ALU.mult, op1=ALU.add).then_inc(lin_used, 1)

                aggregate(1)

                with dve.Fori(0, NCH) as c:
                    for j in range(CH):
                        q = c * CH + j
                        dve.wait_ge(lin_done, q + (Q + 1))
                        v.scalar_tensor_tensor(out=acc[:, :, bass.ds(q * P, P)],
                                               in0=bank(6 + j % 2, D).rearrange("p (c n) -> p c n", c=KC),
                                               scalar=dinv[:, bass.ds(q, 1)],
                                               in1=b2g[:, :].rearrange("p (c n) -> p c n", c=KC),
                                               op0=ALU.mult, op1=ALU.add).then_inc(lin_used, 1)
                dve.wait_ge(sum_done, 1)
                chain(v.tensor_scalar(mean_b[:, :], bank(4, D), 1.0 / N, None, ALU.mult))
                with dve.Fori(0, NCH) as c:
                    for k in range(KC):
                        a = acc[:, k, bass.ds(c * (CH * P), CH * P)].rearrange("p (t n) -> p t n", n=P)
                        v.tensor_tensor(a, a, mean_b[:, k * P:(k + 1) * P].unsqueeze(1).broadcast_to([P, CH, P]),
                                        ALU.subtract).then_inc(centred, 1)
                dve.wait_ge(sum_done, 2)
                v.tensor_scalar(sd_b[:, :], bank(5, D), 1.0 / N, BN_EPS, ALU.mult, ALU.add).then_inc(bn_var, 1)
                dve.wait_ge(bn_sd, 1)
                chain(v.reciprocal(scale_b[:, :], sd_b[:, :]))
                chain(v.tensor_tensor(scale_b[:, :], scale_b[:, :], gam[:, :], ALU.mult))

                for c in range(NCH):
                    n0 = c % 2 * CH * D
                    l3 = tile3(ring[:, n0:n0 + CH * D])
                    conv = [acc[:, k, c * CH * P:(c + 1) * CH * P].rearrange("p (t n) -> p t n", n=P) for k in range(KC)]
                    for k in range(KC):
                        ins = v.tensor_tensor(conv[k], conv[k], scale_b[:, k * P:(k + 1) * P].unsqueeze(1).broadcast_to(
                            [P, CH, P]), ALU.mult)
                    chain(ins)
                    dve.wait_ge(lb_ready, CH * (c + 1))
                    for k in range(KC):
                        ins = v.tensor_tensor(l3[:, :, k * P:(k + 1) * P], l3[:, :, k * P:(k + 1) * P], conv[k], ALU.add)
                    chain(ins)
                    xc = X[:, c * CH * D:(c + 1) * CH * D]
                    chain(v.scalar_tensor_tensor(out=xc, in0=ring[:, n0:n0 + CH * D], scalar=0.0, in1=xc,
                                                 op0=ALU.max, op1=ALU.add))
                    for j in range(CH):
                        ins = v.bn_stats(stats[:, 6 * j:6 * j + 6], xc[:, j * D:(j + 1) * D])
                    ins.then_inc(lb_used, 1)
                    chain(v.tensor_copy(dscr[:, :], zeros[:, 0:1]))
                    for j in range(CH):
                        v.bn_aggr(mv[:, 2 * (c * CH + j):2 * (c * CH + j + 1)], stats[:, 6 * j:6 * j + 6])
                    chain(v.tensor_copy(dscr[:, :], zeros[:, 0:1]))
                    tiles = slice(c * CH, (c + 1) * CH)
                    v.tensor_scalar(rstd[:, tiles], var[:, tiles], LN_EPS, None, ALU.add).then_inc(ln2_var, 1)
                    dve.wait_ge(ln2_sd, c + 1)
                    chain(v.reciprocal(mask[:, tiles], rstd[:, tiles]))
                    chain(v.tensor_copy(rstd[:, tiles], mask[:, tiles]))
                    v.scalar_tensor_tensor(out=nmr[:, tiles], in0=mean[:, tiles], scalar=-1.0, in1=rstd[:, tiles],
                                           op0=ALU.mult, op1=ALU.mult).then_inc(ln2_set, 1)
                def by_tile(ap):
                    return ap[:, :].rearrange("p (t e) -> p t e", e=NX)

                def per_tile(ap):
                    return ap[:, :].unsqueeze(2).broadcast_to([P, NT, NX])

                def per_expert(ap):
                    return ap[:, :].unsqueeze(1).broadcast_to([P, NT, NX])

                def tt(o, i0, i1, op):
                    chain(v.tensor_tensor(o, i0, i1, op))

                dve.wait_ge(logit_done, 1)
                tt(by_tile(prob), bank(2, T8).rearrange("p (t e) -> p t e", e=NX), per_expert(gb), ALU.add)
                chain(v.tensor_reduce(red[:, :], by_tile(prob), AX_X, ALU.max))
                v.tensor_tensor(by_tile(prob), by_tile(prob), per_tile(red), ALU.subtract).then_inc(lmax_set, 1)
                dve.wait_ge(exp_done, 1)
                chain(v.tensor_reduce(red[:, :], by_tile(prob), AX_X, ALU.add))
                chain(v.reciprocal(cw1[:, :], red[:, :]))
                tt(by_tile(prob), by_tile(prob), per_tile(cw1), ALU.mult)
                for sel, cw in ((sel1, cw1), (sel2, cw2)):
                    chain(v.tensor_reduce(cw[:, :], by_tile(prob), AX_X, ALU.max))
                    tt(by_tile(sA), by_tile(prob), per_tile(cw), ALU.is_equal)
                    tt(by_tile(sA), by_tile(sA), per_expert(rank8), ALU.mult)
                    chain(v.tensor_reduce(red[:, :], by_tile(sA), AX_X, ALU.max))
                    k = 0 if sel is sel1 else 2
                    by_choice = choice.rearrange("p (t k) -> p t k", k=4)
                    v.tensor_copy(by_choice[:, :, k], cw[:, :])
                    v.tensor_scalar(by_choice[:, :, k + 1], red[:, :], -1.0, float(NX), ALU.mult, ALU.add)
                    tt(by_tile(sel), by_tile(sA), per_tile(red), ALU.is_equal)
                    if sel is sel1:
                        chain(v.scalar_tensor_tensor(out=prob[:, :], in0=sel1[:, :], scalar=-2.0, in1=prob[:, :],
                                                     op0=ALU.mult, op1=ALU.add))
                v.tensor_copy(dscr[:, :], zeros[:, 0:1]).then_inc(choice_set, 1)
                chain(v.memset(valid[:, :], 1.0))
                chain(v.tensor_scalar(valid[:, NT - 1:NT], not_pad[:, 0:1], 1.0, None, ALU.add))
                tt(sA[:, :], sel1[:, :], sel2[:, :], ALU.add)
                v.tensor_tensor(by_tile(prob), by_tile(sA), per_tile(valid), ALU.mult).then_inc(member_set, 1)
                dve.wait_ge(rank_done, 1)
                chain(v.tensor_copy(sA[:, :], bank(4, T8)))
                now, then, shift = sA, sB, 1
                while shift < NT:
                    v.tensor_copy(then[:, 0:shift * NX], now[:, 0:shift * NX])
                    tt(then[:, shift * NX:T8], now[:, shift * NX:T8], now[:, 0:T8 - shift * NX], ALU.add)
                    now, then, shift = then, now, 2 * shift
                chain(v.tensor_scalar(cap[:, :], now[:, T8 - NX:T8], float(P - 1), None, ALU.add))
                chain(v.tensor_copy(cap_i[:, :], cap[:, :]))
                chain(v.tensor_scalar(cap_i[:, :], cap_i[:, :], -P, None, ALU.bitwise_and))
                chain(v.tensor_copy(endx[:, :], cap_i[:, :]))
                chain(v.tensor_copy(cap[:, :], endx[:, :]))
                for e in range(1, NX):
                    tt(endx[:, e:e + 1], endx[:, e - 1:e], cap[:, e:e + 1], ALU.add)
                tt(capx[:, :], endx[:, :], cap[:, :], ALU.subtract)
                tt(then[:, :], now[:, :], bank(4, T8), ALU.subtract)
                tt(then[:, :], then[:, :], bank(3, T8), ALU.add)
                tt(by_tile(then), by_tile(then), per_expert(capx), ALU.add)
                for k, sel in enumerate((sel1, sel2)):
                    tt(sel[:, :], sel[:, :], then[:, :], ALU.mult)
                    chain(v.tensor_reduce(pos[:, k * NT:(k + 1) * NT], by_tile(sel), AX_X, ALU.add))
                    tt(pos[:, k * NT:(k + 1) * NT], pos[:, k * NT:(k + 1) * NT], valid[:, :], ALU.mult)
                chain(v.tensor_copy(pos_i, pos[:, :]))
                chain(v.tensor_scalar(sel1[:, 0:2 * NT].bitcast(I32), pos_i, P - 1, None, ALU.bitwise_and))
                chain(v.tensor_scalar(sel2[:, 0:2 * NT].bitcast(I32), pos_i, P.bit_length() - 1, None,
                                      ALU.logical_shift_right))
                chain(v.tensor_copy(pos_hi, sel2[:, 0:2 * NT].bitcast(I32)))
                chain(v.tensor_copy(sA[:, 0:2 * NT], sel1[:, 0:2 * NT].bitcast(I32)))
                for k in range(2):
                    chain(v.scalar_tensor_tensor(out=sB[:, k * NT:(k + 1) * NT], in0=sA[:, k * NT:(k + 1) * NT],
                                                 scalar=1.0, in1=valid[:, :], op0=ALU.add, op1=ALU.mult))
                chain(v.tensor_scalar(pos_lo, sB[:, 0:2 * NT], -1.0, None, ALU.add))
                dve.wait_ge(iota7_set, 1)
                for c in range(2 * NCH):
                    if c >= 2:
                        dve.wait_ge(hot_used, c - 1)
                    rows = slice(c * CH, (c + 1) * CH)
                    lo, hi = hot_lo[c % 2], hot_hi[c % 2].rearrange("p (k n t) -> p k n t", k=3, t=CH)
                    v.tensor_tensor(lo.rearrange("p (n t) -> p n t", t=CH), iota7.rearrange("p (n t) -> p n t", t=CH),
                                    pos_lo[:, rows].unsqueeze(1).broadcast_to([P, P, CH]), ALU.is_equal)
                    chain(v.tensor_tensor(hi[:, 0], iota7.rearrange("p (n t) -> p n t", t=CH)[:, 0:FT],
                                          pos_hi[:, rows].unsqueeze(1).broadcast_to([P, FT, CH]), ALU.is_equal))
                    v.tensor_scalar(hot_hi[c % 2][:, CH * FT:2 * CH * FT], hot_hi[c % 2][:, 0:CH * FT], place[:, 0:1],
                                    None, ALU.mult)
                    v.tensor_tensor(hi[:, 2], hi[:, 0], tile_b[:, rows].unsqueeze(1).broadcast_to([P, FT, CH]),
                                    ALU.mult).then_inc(hot_ready, 1)

                chain(v.tensor_scalar(texp_f[:, :], tile_at[:, :], endx[:, 0:1], None, ALU.is_ge))
                for e in range(1, NX - 1):
                    chain(v.scalar_tensor_tensor(out=texp_f[:, :], in0=tile_at[:, :], scalar=endx[:, e:e + 1],
                                                 in1=texp_f[:, :], op0=ALU.is_ge, op1=ALU.add))
                v.tensor_copy(texp_i[:, :], texp_f[:, :]).then_inc(b1_turned, 1)
                dve.wait_ge(slots_done, 1)
                filled, node_lo, node_hi = [bank(5, 3 * FT)[:, k * FT:(k + 1) * FT] for k in range(3)]
                chain(v.tensor_copy(sA[:, 0:FT], node_lo))
                chain(v.scalar_tensor_tensor(out=sB[:, 0:FT], in0=node_hi, scalar=float(P), in1=sA[:, 0:FT],
                                             op0=ALU.mult, op1=ALU.add))
                chain(v.tensor_scalar(sA[:, 0:FT], filled, -1.0, 1.0, ALU.mult, ALU.add))
                chain(v.scalar_tensor_tensor(out=sel1[:, 0:FT], in0=sA[:, 0:FT], scalar=spare[:, 0:1], in1=sB[:, 0:FT],
                                             op0=ALU.mult, op1=ALU.add))
                chain(v.tensor_copy(slot_i, sel1[:, 0:FT]))

                def expert_of(j):
                    return dve.value_load(texp_i[0:1, bass.ds(j, 1)], min_val=0, max_val=NX - 1)

                def take_in(j, u):
                    static = isinstance(j, int)
                    e = expert_of(j)
                    dve.wait_ge(f_turned, j + 1)
                    v.tensor_copy(xsT[:, (u % 2) * D:(u % 2 + 1) * D], bank(u % 2, D)).then_inc(f_copied, 1)
                    for k in range(2):
                        w = u * DX + D + 2 * k
                        v.tensor_scalar(wab[:, k:k + 1], xs[:, w + 1:w + 2], texp_f[:, bass.ds(j, 1)],
                                        xs[:, w:w + 1], ALU.is_equal, ALU.mult).then_inc(row_weights, 1)
                    dve.wait_ge(row_weights, j * 3 + 2)
                    if not static or j >= 4:
                        dve.wait_ge(ys_ready, j - 3)
                    v.tensor_tensor(wcol[:, u:u + 1], wab[:, 0:1], wab[:, 1:2], ALU.add).then_inc(row_weights, 1)
                    dve.wait_ge(row_weights, j * 3 + 3)
                    if not static or j + 4 < FT:
                        v.tensor_copy(pstg[:, u:u + 1], slot_i[:, bass.ds(j + 4, 1)]).then_inc(g_staged, 1)
                    if not static or j >= 2:
                        dve.wait_ge(h_done, j - 1)
                    v.tensor_copy(w1s[:, (u % 2) * KC * H:(u % 2 + 1) * KC * H],
                                  w1e[:, bass.ds(e * (KC * H), KC * H)]).then_inc(w1_staged, 1)

                def ffn_step(j, u):
                    static = isinstance(j, int)
                    if not static or j + 2 < FT:
                        take_in(j + 2, (u + 2) % 4)
                    e = expert_of(j)
                    if not static or j >= 4:
                        dve.wait_ge(added_out, (j - 3) * 16)
                    v.tensor_copy(pstg[:, 4 + u:5 + u], slot_i[:, bass.ds(j, 1)]).then_inc(a_staged, 1)
                    dve.wait_ge(o_done, j + 2)
                    if not static or j >= 2:
                        dve.wait_ge(ys_ready, j - 1)
                    v.tensor_tensor(yb[:, (u % 2) * D:(u % 2 + 1) * D], bank(4 + u % 2, D),
                                    b2e[:, bass.ds(e * D, D)], ALU.add).then_inc(yb_ready, 1)

                for n in range(4):
                    v.tensor_copy(pstg[:, n:n + 1], slot_i[:, n:n + 1]).then_inc(g_staged, 1)
                dve.wait_ge(ld_exp, 16 * 2 * NX)
                take_in(0, 0)
                take_in(1, 1)
                four_by_four(dve, ffn_step)

            @block.tensor
            def _(pe):
                m = nc.tensor
                pe.sem_inc(self_turned, 1)
                pe.sem_inc(sq_used, CH)
                pe.sem_inc(o_done, 1)

                pe.wait_ge(consts_set, 1)

                def turn_edges(n, rows):
                    for b in range(RB):
                        ins = m.transpose(bank(2 * n, EC, 2)[:, b * P:(b + 1) * P], rows[:, b * P:(b + 1) * P], ident[:, :])
                    ins.then_inc(edges_turned, 1)

                pe.wait_ge(edge_f, 1)
                turn_edges(0, dst_rowf)
                pe.wait_ge(dstT_set, 1)
                m.matmul(bank(6, NG), ones[0:1, :], dstT[0:1, 0:ET:GT], start=True, stop=True).then_inc(base_bc, 1)
                turn_edges(1, w_row)
                pe.wait_ge(edge_f, 2)
                turn_edges(2, src_rowf)
                pe.wait_ge(bad_set, 1)
                m.matmul(bank(6, 1), ones[:, :], bad[:, 3:4], start=True, stop=True).then_inc(bad_sum, 1)
                pe.wait_ge(flag_set, 1)
                general = pe.value_load(flag_i[0:1, 0:1], min_val=0, max_val=1)
                pe.wait_ge(ld_const, 16 * 10)
                m.transpose(bank(6, NX * HC), b1rows[0:NX * HC, 0:P], ident[0:NX * HC, 0:NX * HC]).then_inc(b1_turned, 1)

                with pe.If(general == 0):
                    with pe.Fori(0, NG // 2) as i:
                        for h in range(2):
                            pe.wait_ge(lob_ready, i * 2 + (h + 1))
                            hot = lob[:, h * GT * P:(h + 1) * GT * P].rearrange("p (n t) -> p n t", t=GT)
                            for j in range(GT):
                                ins = m.matmul(bank(2 + h, 6), hot[:, :, j],
                                               w_group[:, (h * GT + j) * 6:(h * GT + j + 1) * 6],
                                               start=(j == 0), stop=(j == GT - 1))
                            ins.then_inc(oh_free, 1)
                    pe.wait_ge(deg_summed, 1)
                    m.transpose(bank(0, P)[0:2 * NG, :], deg_cols, ident[:, :])
                    m.transpose(bank(1, P)[0:2 * NG, :], tile_f[:, :], ident[:, :]).then_inc(deg_turned, 1)
                    pe.wait_ge(deg_spread, 1)
                    m.matmul(bank(7, NT), deg_rows[0:2 * NG, :], tile_is[0:2 * NG, :], start=True,
                             stop=True).then_inc(deg_done, 1)
                with pe.Else():
                    m.matmul(bank(7, NT), ident[:, :], zeros[:, 0:NT], start=True, stop=False, skip_group_check=True)
                    with pe.Fori(0, ET // (2 * OH)) as i:
                        for h in range(2):
                            for j in range(OH):
                                n = h * OH + j
                                pe.wait_ge(hi_ready, i * (2 * OH) + (n + 1))
                                ins = m.matmul(bank(7, NT), LO[:, n * P:(n + 1) * P], HI[:, n * NT:(n + 1) * NT],
                                               start=False, stop=False, skip_group_check=True)
                            ins.then_inc(oh_free, 1)
                    m.matmul(bank(7, NT), ident[:, :], zeros[:, 0:NT], start=False, stop=True,
                             skip_group_check=True).then_inc(deg_done, 1)

                def turn_self(layer, n, u, loads):
                    pe.wait_ge(self_in[u], loads)
                    pe.wait_ge(self_added, n + (Q * layer + 1))
                    for k in range(KC):
                        ins = m.transpose(bank(4 + u, D)[:, k * P:(k + 1) * P],
                                          self_rows[:, u * D + k * P:u * D + (k + 1) * P], ident[:, :])
                    ins.then_inc(self_turned, 1)

                def aggregate(layer):
                    pe.wait_ge(sc_set, 1)
                    turn_self(layer, 0, 0, 16 * ((OWN + 1) * layer + 1))
                    with pe.If(general == 0):
                        def group(i, h, own):
                            k = i * 2 + h
                            if own:
                                u = (h + 1) % 2
                                turn_self(layer, k + 1, u, i * 16 + 16 * ((OWN + 1 - u) * layer + (2 - u)))
                            pe.wait_ge(added, k + (NG * layer + 1))
                            for j in range(GT):
                                n = h * GT + j
                                pe.wait_ge(s_ready, i * (2 * GT) + (ET * layer + n + 1))
                                pe.wait_ge(gathered[n], i * 16 + (16 * (NG // 2) * layer + 16))
                                for c in range(KC):
                                    ins = m.matmul(bank(2 * h + c, P), G[:, n * D + c * P:n * D + (c + 1) * P],
                                                   S[:, n * P:(n + 1) * P], start=(j == 0), stop=(j == GT - 1))
                            ins.then_inc(summed, 1)

                        with pe.Fori(0, OWN) as i:
                            for h in range(2):
                                group(i, h, True)
                        with pe.Fori(OWN, NG // 2) as i:
                            for h in range(2):
                                group(i, h, False)
                    with pe.Else():
                        with pe.Fori(0, OWN) as i:
                            for h in range(2):
                                u = (h + 1) % 2
                                turn_self(layer, i * 2 + (h + 1), u, i * 16 + 16 * ((OWN + 1 - u) * layer + (2 - u)))
                        with pe.Fori(0, ET) as i:
                            pe.wait_ge(gen_gathered, i * 16 + (16 * ET * layer + 16))
                            for w in range(NW):
                                pe.wait_ge(gen_s, i * NW + (ET * NW * layer + w + 1))
                                pe.wait_ge(gen_added, i * NW + (ET * NW * layer + w + 1))
                                for c in range(KC):
                                    ins = m.matmul(bank(c, WIN), G[:, c * P:(c + 1) * P], S[:, 0:WIN],
                                                   start=True, stop=True)
                                ins.then_inc(gen_summed, 1)
                    pe.wait_ge(agg_done, layer + 1)

                def linear(layer, q, j, W):
                    pe.wait_ge(lin_used, prior(q, j) + Q * layer)
                    for k in range(KC):
                        ins = m.matmul(bank(6 + j % 2, D), acc[:, k, bass.ds(q * P, P)], W[:, k * D:(k + 1) * D],
                                       start=(k == 0), stop=(k == KC - 1))
                    ins.then_inc(lin_done, 1)

                aggregate(0)
                for c in range(NCH):
                    for j in range(CH):
                        linear(0, CH * c + j, j, W1g)
                aggregate(1)

                acc_sum, acc_sq = bank(4, D), bank(5, D)

                def add_up(total, lhs, rhs, first=False, last=False):
                    return m.matmul(total.rearrange("p (c n) -> p c n", c=KC), lhs[:, :], rhs,
                                    start=first, stop=last, skip_group_check=True)

                z3 = zeros[:, :].rearrange("p (c n) -> p c n", c=KC)
                for c in range(NCH):
                    for j in range(CH):
                        q = c * CH + j
                        linear(1, q, j, W2g)
                pe.wait_ge(z_added, 1 + NT)
                for n in range(2):
                    add_up(acc_sum, ones, tmp[:, n * D:(n + 1) * D].rearrange("p (c n) -> p c n", c=KC), first=(n == 0))
                add_up(acc_sum, not_pad, acc[:, :, (NT - 1) * P:NT * P], last=True).then_inc(sum_done, 1)
                add_up(acc_sq, ones, z3, first=True)
                with pe.Fori(0, NCH) as c:
                    for j in range(CH):
                        pe.wait_ge(sq_ready, c * CH + (j + 1))
                        add_up(acc_sq, ones, slot(j).rearrange("p (c n) -> p c n", c=KC)).then_inc(sq_used, 1)
                add_up(acc_sq, not_pad, slot(CH - 1).rearrange("p (c n) -> p c n", c=KC), last=True).then_inc(sum_done, 1)

                for c in range(NCH):
                    for j in range(CH):
                        q = c * CH + j
                        pe.wait_ge(n_ready, q + 1)
                        if c:
                            pe.wait_ge(n_copied, q - CH + 1)
                        for k in range(KC):
                            ins = m.transpose(turned(j)[:, k * P:(k + 1) * P], acc[:, k, q * P:(q + 1) * P], ident[:, :])
                        ins.then_inc(n_turned, 1)
                    for q in range(c * CH, (c + 1) * CH):
                        pe.wait_ge(n_copied, q + 1)
                        for k in range(KC):
                            m.matmul(bank(2, T8)[:, q * NX:(q + 1) * NX], acc[:, k, q * P:(q + 1) * P],
                                     gw[:, k * NX:(k + 1) * NX], start=(k == 0), stop=(k == KC - 1))
                m.matmul(bank(3, 8), ident[:, :], zeros[:, 0:8], start=True, stop=True).then_inc(logit_done, 1)

                pe.wait_ge(member_set, 1)
                m.matmul(bank(3, T8), before[:, :], prob[:, :], start=True, stop=True)
                m.matmul(bank(4, T8), ones[:, :], prob[:, :], start=True, stop=True).then_inc(rank_done, 1)

                for c in range(2 * NCH):
                    pe.wait_ge(hot_ready, c + 1)
                    lo = hot_lo[c % 2].rearrange("p (n t) -> p n t", t=CH)
                    hi = hot_hi[c % 2].rearrange("p (n t) -> p n t", t=CH)
                    for j in range(CH):
                        ins = m.matmul(bank(5, 3 * FT), lo[:, :, j], hi[:, :, j], start=(c + j == 0),
                                       stop=(c == 2 * NCH - 1 and j == CH - 1))
                    ins.then_inc(hot_used, 1)
                m.matmul(bank(3, 8), ident[:, :], zeros[:, 0:8], start=True, stop=True).then_inc(slots_done, 1)

                pe.wait_ge(b1_turned, 2)
                pe.wait_ge(ld_exp, 16 * 2 * NX)

                def expert_of(j):
                    return pe.value_load(texp_i[0:1, bass.ds(j, 1)], min_val=0, max_val=NX - 1)

                def turn_x(j, s4, turn_of_slot):
                    pe.wait_ge(xs_in[s4], turn_of_slot)
                    for k in range(KC):
                        ins = m.transpose(bank(s4 % 2, D)[:, k * P:(k + 1) * P],
                                          xs[:, s4 * DX + k * P:s4 * DX + (k + 1) * P], ident[:, :])
                    ins.then_inc(f_turned, 1)

                def hidden(j, s):
                    pe.wait_ge(w1_staged, j + 1)
                    pe.wait_ge(f_copied, j + 1)
                    for c in range(HC):
                        for k in range(KC):
                            ins = m.matmul(psum[:, 2 + s, c * P:(c + 1) * P],
                                           w1s[:, s * KC * H + k * H + c * P:s * KC * H + k * H + (c + 1) * P],
                                           xsT[:, s * D + k * P:s * D + (k + 1) * P], start=(k == 0), stop=(k == KC - 1))
                    ins.then_inc(h_done, 1)

                def output(j, s, e):
                    pe.wait_ge(h_act, j + 1)
                    for c in range(HC):
                        ins = m.matmul(bank(4 + s, D), hT[:, s * H + c * P:s * H + (c + 1) * P],
                                       w2e[:, bass.ds(e * (HC * D) + c * D, D)], start=(c == 0), stop=(c == HC - 1))
                    ins.then_inc(o_done, 1)

                turn_x(0, 0, 16)
                turn_x(1, 1, 16)
                hidden(0, 0)

                def ffn_step(j, u):
                    static = isinstance(j, int)
                    e = expert_of(j)
                    if not static or j + 2 < FT:
                        into = (u + 2) % 4
                        turn_x(j + 2, into, (j + 2) // 4 * 16 + 16 if static else (j - u) * 4 + 16 * ((u + 2) // 4 + 1))
                    if not static or j + 1 < FT:
                        hidden(j + 1, (u + 1) % 2)
                    if not static or j >= 2:
                        pe.wait_ge(yb_ready, j - 1)
                    output(j, u % 2, e)

                four_by_four(pe, ffn_step)


_INS = ['x', 'src', 'dst', 'edge_weight', 'L0_gnn_W1', 'L0_gnn_b1', 'L0_gnn_W2', 'L0_gnn_b2', 'L0_gnn_gamma',
        'L0_gnn_beta', 'L0_ffn_gate_w', 'L0_ffn_gate_b', 'L0_ffn_W1', 'L0_ffn_b1', 'L0_ffn_W2', 'L0_ffn_b2']
_OUTS = [((6250, 256), 'float32')]


def kernel(**inputs):
    import numpy as _np
    import concourse.bacc as _bacc
    from concourse import mybir as _mybir
    from concourse.bass_utils import run_bass_kernel_spmd as _run

    nc = _bacc.Bacc("TRN2", target_bir_lowering=False, num_devices=1)
    arrays, args = {}, []
    for name in _INS:
        a = _np.ascontiguousarray(inputs[name])
        arrays[f"in_{name}_dram"] = a
        args.append(nc.dram_tensor(f"in_{name}_dram", a.shape, _mybir.dt.from_np(a.dtype), kind="ExternalInput").ap())
    for i, (shape, dtype) in enumerate(_OUTS):
        dt = _mybir.dt.from_np(_np.dtype(dtype))
        args.append(nc.dram_tensor(f"out_{i}_dram", shape, dt, kind="ExternalOutput").ap())
    gnn_ffn(nc, *args)
    r = _run(nc, [arrays], core_ids=[0])
    return r.results[0]["out_0_dram"]
```
